# Optimizing a Trainium2 kernel written in Bass

```python
import numpy as np
import jax
import jax.numpy as jnp

def _softmax(x, axis=-1):
    return jax.nn.softmax(x, axis=axis)

def _gelu(x):
    return jax.nn.gelu(x, approximate=True)

def _silu(x):
    return jax.nn.silu(x)

def _sigmoid(x):
    return jax.nn.sigmoid(x)

def _layernorm(x, axis=-1, eps=1e-05):
    m = jnp.mean(x, axis=axis, keepdims=True)
    v = jnp.var(x, axis=axis, keepdims=True)
    return (x - m) / jnp.sqrt(v + eps)

def _scatter_add(tgt, idx, src, axis=0):
    return tgt.at[idx].add(src)

def _segment_sum(src, seg, n):
    return jax.ops.segment_sum(src, seg, n)
kernel_name = 'mk_conv_seq_d4_conv_nchw256_r2_39f99b'

def setup_inputs(seed: int=0):
    np.random.seed(seed)
    _w = jnp.asarray

    def _rec_inputs():
        import jax
        import jax.numpy as jnp
        _gk = jax.random.key(seed)
        x = -0.000125 + 0.9999 * jax.random.normal(jax.random.fold_in(_gk, 1), (32, 128, 32, 32), jnp.float32)
        return x
    x = _rec_inputs()

    def _L0_conv_setup():
        import jax, jax.numpy as jnp
        import numpy as np
        EPS = 1e-05
        key = jax.random.key(seed)
        k1, k2, k3 = jax.random.split(key, 3)
        B, C, H, W = (32, 128, 32, 32)
        F = C // 4
        x = jax.random.normal(k1, (B, C, H, W), dtype=jnp.float32)
        weight = jnp.eye(4, dtype=jnp.float32)[:, :, None] * jnp.ones((F,), jnp.float32) + 0.1 * jax.random.normal(k2, (4, 4, F), dtype=jnp.float32)
        bias = 0.1 * jax.random.normal(k3, (4, F), dtype=jnp.float32)
        return {'x': x, 'weight': weight, 'bias': bias}
    _L0_conv_all = _L0_conv_setup()
    _L0_conv_in = {k: v for k, v in _L0_conv_all.items() if k in ('weight', 'bias')}
    del _L0_conv_all

    def _L1_conv_setup():
        import jax, jax.numpy as jnp
        import numpy as np
        B, C, H, W = (4, 128, 32, 32)
        D_STATE, D_CONV, EXPAND = (16, 4, 2)
        D_INNER = EXPAND * C
        DT_RANK = (C + 15) // 16

        def _mamba2conv(x, ln_w, ln_b, W_in, conv_w, conv_b, W_x, W_dt, b_dt, A_log, Dp, W_out):
            b, c, h, w = x.shape
            L = h * w
            xf = x.reshape(b, c, L).transpose(0, 2, 1)
            mu = jnp.mean(xf, axis=-1, keepdims=True)
            var = jnp.var(xf, axis=-1, keepdims=True)
            xn = (xf - mu) * jax.lax.rsqrt(var + 1e-05) * ln_w + ln_b
            xz = jnp.einsum('blc,ec->ble', xn, W_in)
            xi, z = jnp.split(xz, 2, axis=-1)
            d_conv = conv_w.shape[1]
            xp = jnp.pad(xi, ((0, 0), (d_conv - 1, 0), (0, 0)))
            xc = conv_b
            for k in range(d_conv):
                xc = xc + xp[:, k:k + L, :] * conv_w[:, k]
            xc = jax.nn.silu(xc)
            dbl = jnp.einsum('bld,ed->ble', xc, W_x)
            dt_rank = W_dt.shape[1]
            n = A_log.shape[1]
            dt, Bm, Cm = jnp.split(dbl, [dt_rank, dt_rank + n], axis=-1)
            delta = jax.nn.softplus(jnp.einsum('blr,dr->bld', dt, W_dt) + b_dt)
            A = -jnp.exp(A_log)

            def step(hst, xs):
                d_t, B_t, C_t, u_t = xs
                dA = jnp.exp(d_t[:, :, None] * A)
                hst = hst * dA + (d_t * u_t)[:, :, None] * B_t[:, None, :]
                y_t = jnp.einsum('bdn,bn->bd', hst, C_t)
                return (hst, y_t)
            h0 = jnp.zeros((b, W_dt.shape[0], n), xc.dtype)
            xs = (delta.transpose(1, 0, 2), Bm.transpose(1, 0, 2), Cm.transpose(1, 0, 2), xc.transpose(1, 0, 2))
            _, ys = jax.lax.scan(step, h0, xs)
            y = ys.transpose(1, 0, 2) + xc * Dp
            y = y * jax.nn.silu(z)
            out = jnp.einsum('bld,cd->blc', y, W_out)
            out = out.transpose(0, 2, 1).reshape(b, c, h, w)
            return out + x
        key = jax.random.key(seed)
        ks = jax.random.split(key, 12)
        x = jax.random.normal(ks[0], (B, C, H, W), jnp.float32)
        ln_w = jnp.ones((C,), jnp.float32)
        ln_b = jnp.zeros((C,), jnp.float32)
        s = 1.0 / np.sqrt(C)
        W_in = jax.random.normal(ks[1], (2 * D_INNER, C), jnp.float32) * s
        conv_w = jax.random.normal(ks[2], (D_INNER, D_CONV), jnp.float32) * 0.5
        conv_b = jnp.zeros((D_INNER,), jnp.float32)
        si = 1.0 / np.sqrt(D_INNER)
        W_x = jax.random.normal(ks[3], (DT_RANK + 2 * D_STATE, D_INNER), jnp.float32) * si
        W_dt = jax.random.normal(ks[4], (D_INNER, DT_RANK), jnp.float32) * (1.0 / np.sqrt(DT_RANK))
        b_dt = jax.random.uniform(ks[5], (D_INNER,), jnp.float32, -4.0, -2.0)
        A_log = jnp.log(jnp.broadcast_to(jnp.arange(1, D_STATE + 1, dtype=jnp.float32), (D_INNER, D_STATE)))
        Dp = jnp.ones((D_INNER,), jnp.float32)
        W_out = jax.random.normal(ks[6], (C, D_INNER), jnp.float32) * si
        return {'x': x, 'ln_w': ln_w, 'ln_b': ln_b, 'W_in': W_in, 'conv_w': conv_w, 'conv_b': conv_b, 'W_x': W_x, 'W_dt': W_dt, 'b_dt': b_dt, 'A_log': A_log, 'Dp': Dp, 'W_out': W_out}
    _L1_conv_all = _L1_conv_setup()
    _L1_conv_in = {k: v for k, v in _L1_conv_all.items() if k in ('ln_w', 'ln_b', 'W_in', 'conv_w', 'conv_b', 'W_x', 'W_dt', 'b_dt', 'A_log', 'Dp', 'W_out')}
    del _L1_conv_all

    def _L2_conv_setup():
        import jax, jax.numpy as jnp
        import numpy as np
        B, C, H, W = (4, 128, 32, 32)
        key = jax.random.key(seed)
        ks = jax.random.split(key, 8)
        s = 0.02
        return {'x': jax.random.normal(ks[0], (B, C, H, W), dtype=jnp.float32), 'Wq': jax.random.normal(ks[1], (C, C), dtype=jnp.float32) * s, 'bq': jax.random.normal(ks[2], (C,), dtype=jnp.float32) * s, 'Wk': jax.random.normal(ks[3], (C, C), dtype=jnp.float32) * s, 'bk': jax.random.normal(ks[4], (C,), dtype=jnp.float32) * s, 'Wv': jax.random.normal(ks[5], (C, C), dtype=jnp.float32) * s, 'bv': jax.random.normal(ks[6], (C,), dtype=jnp.float32) * s, 'gamma': jax.random.normal(ks[7], (1,), dtype=jnp.float32)}
    _L2_conv_all = _L2_conv_setup()
    _L2_conv_in = {k: v for k, v in _L2_conv_all.items() if k in ('Wq', 'bq', 'Wk', 'bk', 'Wv', 'bv', 'gamma')}
    del _L2_conv_all

    def _L3_conv_setup():
        import jax, jax.numpy as jnp
        import numpy as np
        N, C, H, W = (32, 128, 32, 32)
        BN_EPS = 1e-05
        key = jax.random.key(seed)
        k = jax.random.split(key, 4)
        x = jax.random.normal(k[0], (N, C, H, W), jnp.float32)
        theta_w = jax.random.normal(k[1], (C // 2, C), jnp.float32) / np.sqrt(C).astype(np.float32)
        phi_w = jax.random.normal(k[2], (C // 2, C), jnp.float32) / np.sqrt(C).astype(np.float32)
        conv_w = jax.random.normal(k[3], (C, C), jnp.float32) / np.sqrt(C).astype(np.float32)
        gamma = jnp.ones((C,), jnp.float32)
        beta = jnp.zeros((C,), jnp.float32)
        return {'x': x, 'theta_w': theta_w, 'phi_w': phi_w, 'conv_w': conv_w, 'gamma': gamma, 'beta': beta}
    _L3_conv_all = _L3_conv_setup()
    _L3_conv_in = {k: v for k, v in _L3_conv_all.items() if k in ('theta_w', 'phi_w', 'conv_w', 'gamma', 'beta')}
    del _L3_conv_all
    return {'x': x, 'L0_conv_weight': _L0_conv_in['weight'], 'L0_conv_bias': _L0_conv_in['bias'], 'L1_conv_ln_w': _L1_conv_in['ln_w'], 'L1_conv_ln_b': _L1_conv_in['ln_b'], 'L1_conv_W_in': _L1_conv_in['W_in'], 'L1_conv_conv_w': _L1_conv_in['conv_w'], 'L1_conv_conv_b': _L1_conv_in['conv_b'], 'L1_conv_W_x': _L1_conv_in['W_x'], 'L1_conv_W_dt': _L1_conv_in['W_dt'], 'L1_conv_b_dt': _L1_conv_in['b_dt'], 'L1_conv_A_log': _L1_conv_in['A_log'], 'L1_conv_Dp': _L1_conv_in['Dp'], 'L1_conv_W_out': _L1_conv_in['W_out'], 'L2_conv_Wq': _L2_conv_in['Wq'], 'L2_conv_bq': _L2_conv_in['bq'], 'L2_conv_Wk': _L2_conv_in['Wk'], 'L2_conv_bk': _L2_conv_in['bk'], 'L2_conv_Wv': _L2_conv_in['Wv'], 'L2_conv_bv': _L2_conv_in['bv'], 'L2_conv_gamma': _L2_conv_in['gamma'], 'L3_conv_theta_w': _L3_conv_in['theta_w'], 'L3_conv_phi_w': _L3_conv_in['phi_w'], 'L3_conv_conv_w': _L3_conv_in['conv_w'], 'L3_conv_gamma': _L3_conv_in['gamma'], 'L3_conv_beta': _L3_conv_in['beta']}

def reference(x, L0_conv_weight, L0_conv_bias, L1_conv_ln_w, L1_conv_ln_b, L1_conv_W_in, L1_conv_conv_w, L1_conv_conv_b, L1_conv_W_x, L1_conv_W_dt, L1_conv_b_dt, L1_conv_A_log, L1_conv_Dp, L1_conv_W_out, L2_conv_Wq, L2_conv_bq, L2_conv_Wk, L2_conv_bk, L2_conv_Wv, L2_conv_bv, L2_conv_gamma, L3_conv_theta_w, L3_conv_phi_w, L3_conv_conv_w, L3_conv_gamma, L3_conv_beta):
    import jax
    import jax.numpy as jnp

    def _L0_conv_ref(x, weight, bias):
        import jax, jax.numpy as jnp
        import numpy as np
        EPS = 1e-05
        B, C, H, W = x.shape
        F = C // 4
        xq = x.reshape(B, 4, F, H, W).transpose(1, 0, 2, 3, 4)
        mean = xq.mean(axis=(1, 3, 4))
        xc = xq - mean[:, None, :, None, None]
        N = B * H * W
        v = xc.transpose(2, 0, 1, 3, 4).reshape(F, 4, N)
        cov = jnp.einsum('fin,fjn->fij', v, v) / N
        L = jnp.linalg.cholesky(cov + EPS * jnp.eye(4, dtype=x.dtype))
        z = jax.scipy.linalg.solve_triangular(L, v, lower=True)
        z = z.reshape(F, 4, B, H, W).transpose(1, 2, 0, 3, 4)
        out = jnp.einsum('ijf,jbfhw->ibfhw', weight, z) + bias[:, None, :, None, None]
        return out.transpose(1, 0, 2, 3, 4).reshape(B, C, H, W)

    def _L1_conv_ref(x, ln_w, ln_b, W_in, conv_w, conv_b, W_x, W_dt, b_dt, A_log, Dp, W_out):
        import jax, jax.numpy as jnp
        import numpy as np
        B, C, H, W = (4, 128, 32, 32)
        D_STATE, D_CONV, EXPAND = (16, 4, 2)
        D_INNER = EXPAND * C
        DT_RANK = (C + 15) // 16

        def _mamba2conv(x, ln_w, ln_b, W_in, conv_w, conv_b, W_x, W_dt, b_dt, A_log, Dp, W_out):
            b, c, h, w = x.shape
            L = h * w
            xf = x.reshape(b, c, L).transpose(0, 2, 1)
            mu = jnp.mean(xf, axis=-1, keepdims=True)
            var = jnp.var(xf, axis=-1, keepdims=True)
            xn = (xf - mu) * jax.lax.rsqrt(var + 1e-05) * ln_w + ln_b
            xz = jnp.einsum('blc,ec->ble', xn, W_in)
            xi, z = jnp.split(xz, 2, axis=-1)
            d_conv = conv_w.shape[1]
            xp = jnp.pad(xi, ((0, 0), (d_conv - 1, 0), (0, 0)))
            xc = conv_b
            for k in range(d_conv):
                xc = xc + xp[:, k:k + L, :] * conv_w[:, k]
            xc = jax.nn.silu(xc)
            dbl = jnp.einsum('bld,ed->ble', xc, W_x)
            dt_rank = W_dt.shape[1]
            n = A_log.shape[1]
            dt, Bm, Cm = jnp.split(dbl, [dt_rank, dt_rank + n], axis=-1)
            delta = jax.nn.softplus(jnp.einsum('blr,dr->bld', dt, W_dt) + b_dt)
            A = -jnp.exp(A_log)

            def step(hst, xs):
                d_t, B_t, C_t, u_t = xs
                dA = jnp.exp(d_t[:, :, None] * A)
                hst = hst * dA + (d_t * u_t)[:, :, None] * B_t[:, None, :]
                y_t = jnp.einsum('bdn,bn->bd', hst, C_t)
                return (hst, y_t)
            h0 = jnp.zeros((b, W_dt.shape[0], n), xc.dtype)
            xs = (delta.transpose(1, 0, 2), Bm.transpose(1, 0, 2), Cm.transpose(1, 0, 2), xc.transpose(1, 0, 2))
            _, ys = jax.lax.scan(step, h0, xs)
            y = ys.transpose(1, 0, 2) + xc * Dp
            y = y * jax.nn.silu(z)
            out = jnp.einsum('bld,cd->blc', y, W_out)
            out = out.transpose(0, 2, 1).reshape(b, c, h, w)
            return out + x
        return _mamba2conv(x, ln_w, ln_b, W_in, conv_w, conv_b, W_x, W_dt, b_dt, A_log, Dp, W_out)

    def _L2_conv_ref(x, Wq, bq, Wk, bk, Wv, bv, gamma):
        import jax, jax.numpy as jnp
        import numpy as np
        B, C, H, W = (4, 128, 32, 32)
        b, c, h, w = x.shape
        n = h * w
        xf = x.reshape(b, c, n)
        q = jnp.einsum('oc,bcn->bon', Wq, xf) + bq[None, :, None]
        k = jnp.einsum('oc,bcn->bon', Wk, xf) + bk[None, :, None]
        v = jnp.einsum('oc,bcn->bon', Wv, xf) + bv[None, :, None]
        energy = jnp.einsum('bci,bcj->bij', q, k)
        attention = jax.nn.softmax(energy, axis=-1)
        out = jnp.einsum('bcj,bij->bci', v, attention)
        out = gamma[0] * out + xf
        return out.reshape(b, c, h, w)

    def _L3_conv_ref(x, theta_w, phi_w, conv_w, gamma, beta):
        import jax, jax.numpy as jnp
        import numpy as np
        N, C, H, W = (32, 128, 32, 32)
        BN_EPS = 1e-05
        n, c, h, w = x.shape
        hw = h * w
        theta = jnp.einsum('nchw,dc->ndhw', x, theta_w).reshape(n, c // 2, hw)
        phi = jnp.einsum('nchw,dc->ndhw', x, phi_w).reshape(n, c // 2, hw)
        g = x.reshape(n, c, hw)
        scores = jnp.einsum('nia,nib->nab', theta, phi) / jnp.sqrt(jnp.float32(c))
        attn = jax.nn.softmax(scores, axis=-1)
        f = jnp.einsum('nab,nib->nia', attn, g).reshape(n, c, h, w)
        f = jnp.einsum('nchw,dc->ndhw', f, conv_w)
        mean = jnp.mean(f, axis=(0, 2, 3), keepdims=True)
        var = jnp.mean(jnp.square(f - mean), axis=(0, 2, 3), keepdims=True)
        f = (f - mean) * jax.lax.rsqrt(var + BN_EPS)
        f = f * gamma[None, :, None, None] + beta[None, :, None, None]
        return f + x

    def _gn(v, G=32, eps=1e-05):
        B_, C_, H_, W_ = v.shape
        g = v.reshape(B_, G, C_ // G, H_, W_)
        m = jnp.mean(g, axis=(2, 3, 4), keepdims=True)
        s = jnp.var(g, axis=(2, 3, 4), keepdims=True)
        return ((g - m) / jnp.sqrt(s + eps)).reshape(v.shape)

    def _ln_c(v, eps=1e-06):
        m = jnp.mean(v, axis=1, keepdims=True)
        s = jnp.var(v, axis=1, keepdims=True)
        return (v - m) / jnp.sqrt(s + eps)

    def _ln_t(v, eps=1e-05):
        m = jnp.mean(v, axis=-1, keepdims=True)
        s = jnp.var(v, axis=-1, keepdims=True)
        return (v - m) / jnp.sqrt(s + eps)

    def _to_tokens(v):
        B_, C_, H_, W_ = v.shape
        return v.reshape(B_, C_, H_ * W_).transpose(0, 2, 1)

    def _from_tokens(t, like):
        B_, C_, H_, W_ = like.shape
        return t.transpose(0, 2, 1).reshape(B_, C_, H_, W_)
    x = _L0_conv_ref(x, L0_conv_weight, L0_conv_bias)
    x = _L1_conv_ref(x, L1_conv_ln_w, L1_conv_ln_b, L1_conv_W_in, L1_conv_conv_w, L1_conv_conv_b, L1_conv_W_x, L1_conv_W_dt, L1_conv_b_dt, L1_conv_A_log, L1_conv_Dp, L1_conv_W_out)
    x = _L2_conv_ref(x, L2_conv_Wq, L2_conv_bq, L2_conv_Wk, L2_conv_bk, L2_conv_Wv, L2_conv_bv, L2_conv_gamma)
    x = _L3_conv_ref(x, L3_conv_theta_w, L3_conv_phi_w, L3_conv_conv_w, L3_conv_gamma, L3_conv_beta)
    return x

_drawn_inputs = setup_inputs


def setup_inputs(seed=0):
    import zlib

    import numpy as np

    out = dict(_drawn_inputs(seed))
    spreads = {'L1_conv_ln_w': (1.0, 0.2),
     'L1_conv_ln_b': (0.0, 0.1),
     'L1_conv_conv_b': (0.0, 0.1),
     'L1_conv_Dp': (1.0, 0.2),
     'L3_conv_gamma': (1.0, 0.2),
     'L3_conv_beta': (0.0, 0.1)}
    factors = {'L2_conv_Wq': 8.0,
     'L2_conv_bq': 8.0,
     'L2_conv_Wk': 8.0,
     'L2_conv_bk': 64.0,
     'L2_conv_Wv': 8.0,
     'L2_conv_bv': 58.932}
    for name, (base, spread) in spreads.items():
        noise = np.random.default_rng([zlib.crc32(name.encode()), seed]).standard_normal(out[name].shape)
        drawn = base * np.exp(spread * noise) if base else spread * noise
        out[name] = jnp.asarray(drawn.astype(out[name].dtype))
    for name, factor in factors.items():
        out[name] = (out[name] * factor).astype(out[name].dtype)
    return out
```

```python
from contextlib import ExitStack

import concourse.bass as bass
from concourse import mybir

NB, C, HH, WW = 32, 128, 32, 32
L = HH * WW
F = C // 4
DI = 2 * C
NH = DI // C
NS = 16
KC = 4
DR = C // 16
CH = 512
NCH = L // CH
BCR = 2 * NS
NROW = 3 * BCR
TB = L // 128
HD = C // 2
STEPS = NCH * NS
TILES = TB
EPS0, EPS_LN, EPS_BN = 1e-5, 1e-5, 1e-5


def build(nc, x, w0, b0, ln_w, ln_b, w_in, conv_w, conv_b, w_x, w_dt, b_dt, a_log, dp, w_out,
          w_q, b_q, w_k, b_k, w_v, b_v, gam, th_w, ph_w, cv_w, bn_g, bn_b, out):
    fp32, bf16 = mybir.dt.float32, mybir.dt.bfloat16
    ALU = mybir.AluOpType
    ACT = mybir.ActivationFunctionType
    AX = mybir.AxisListType.X
    ctx = ExitStack()
    with ctx:
        def sb(name, shape, dt=fp32):
            return ctx.enter_context(nc.sbuf_tensor(name, shape, dt))

        def pb(name, shape):
            return ctx.enter_context(nc.psum_tensor(name, shape, fp32))

        def sem(name):
            return ctx.enter_context(nc.semaphore(name))

        x2_dram = nc.dram_tensor("x2_scratch", [NB, C, L], fp32).ap()
        f_dram = nc.dram_tensor("f_scratch", [NB, C, L], fp32).ap()

        ident = sb("ident", [128, 128])
        mask32 = sb("mask32", [128, 32])
        sel = sb("sel", [128, BCR, 128], bf16)
        cent = sb("cent", [128, 128])
        avg = sb("avg", [128, 128])
        m0 = sb("m0", [128, 128])
        w_in_t = sb("w_in_t", [128, 2 * DI])
        w_x_t = sb("w_x_t", [128, NH, NROW + DR])
        w_dt_t = sb("w_dt_t", [128, DI])
        w_out_t = sb("w_out_t", [128, NH, C])
        w_q_t = sb("w_q_t", [128, C])
        w_k_t = sb("w_k_t", [128, C])
        w_v_t = sb("w_v_t", [128, C])
        th_t = sb("th_t", [128, HD])
        ph_t = sb("ph_t", [128, HD])
        cv_t = sb("cv_t", [128, C])
        dp_diag = sb("dp_diag", [128, NH, 128])
        cvec = sb("cvec", [128, 32])
        neg_a = sb("neg_a", [128, NH, NS])
        taps = sb("taps", [128, NH, KC])
        (c_b0, c_lnw, c_lnb, c_bq, c_bk, c_bv, c_gam, c_bng, c_bnb, c_c0, c_nshift, c_mean, c_gbv,
         c_s, c_t, c_v, c_rs, c_v2) = (cvec[:, i:i + 1] for i in range(18))
        c_cb, c_bdt, c_dp = (cvec[:, 18 + 2 * i:20 + 2 * i] for i in range(3))
        c_wb = cvec[:, 24:28]

        sums = sb("sums", [128, NB])
        gram = sb("gram", [128, 128])
        dcov = sb("dcov", [128, 5])
        q0 = sb("q0", [32, 96])
        w0s = sb("w0s", [32, 4, 4])
        wcol = sb("wcol", [128, 4])

        xin = sb("xin", [128, L])
        x0 = sb("x0", [128, L])
        ta1 = sb("ta1", [128, L])
        ta2 = sb("ta2", [128, L])
        xn = sb("xn", [128, L])
        xi = sb("xi", [128, NH, KC - 1 + L])
        xc = sb("xc", [128, NH, L])
        sz = sb("sz", [128, NH, L])
        delta = sb("delta", [128, NH, L])
        du = sb("du", [128, NH, L])
        bc = sb("bc", [128, L], bf16)
        mid = sb("mid", [128, L], bf16)
        da = sb("da", [128, 2, NH, CH])
        dbu = sb("dbu", [128, 2, NH, CH])
        hs = sb("hs", [128, 2, NH, CH])
        hlast = sb("hlast", [128, NS, NH])
        cs = sb("cs", [128, 2, CH])
        pa = sb("pa", [128, 2, NH, CH])
        pc = sb("pc", [128, NH, CH])
        x1 = sb("x1", [128, L])
        x1g = sb("x1g", [128, L])
        qa = sb("qa", [128, L])
        ka = sb("ka", [128, L])
        va = sb("va", [128, TB, C])
        p = sb("p", [128, 2, L])
        pt = sb("pt", [128, TB, CH])
        rb = sb("rb", [128, CH])
        fa = sb("fa", [128, L])
        x2 = sb("x2", [128, L])
        nm = sb("nm", [128, 2])
        rsum = sb("rsum", [128, 8])
        rinv = sb("rinv", [128, 4])
        bst = sb("bst", [128, NB, 2, 6])
        mv = sb("mv", [128, 2])
        g = du
        sp_e = [ta1[:, :], p[:, 0, :]]
        sp_l = [ta2[:, :], xn[:, :]]
        rem2 = p[:, 1, :]
        dts = p[:, 1, :]
        fbuf = [xin[:, :], x0[:, :]]
        xbuf = [x1[:, :], x2[:, :]]

        psE = pb("psE", [128, L])
        psY = pb("psY", [128, 2, CH])
        psB = pb("psB", [128, 2, CH])
        psT = pb("psT", [128, 2, CH])

        def flat(t):
            return t[:, :, :].rearrange("p a n -> p (a n)")

        def split(t):
            return flat(t).rearrange("p (j n) -> p j n", j=TB)

        S = {}

        def s(name):
            if name not in S:
                S[name] = sem(name)
            return S[name]

        for name in ("weights_in", "consts_made", "setup_chain", "mean0", "stats_chain", "stats_act",
                     "xl0", "xl1", "st_centred", "st_turned", "st_copied", "st_gram", "st_added",
                     "x_in", "x2_out", "f_out", "fin_chain", "fin_act", "pe_setup",
                     "fscaled", "fsum", "fl0", "fl1", "out0", "out1"):
            s(name)

        PER = dict(
            x0_mm=1, x0_ok=1, cent_mm=1, sq_ok=1, var_mm=1, lnv_ok=1, rs_ok=1, xn_ok=1, xi_mm=2, z_mm=2,
            xi_ok=2, z_ok=2, conv=8, xc_ok=2, dbl_mm=1, dt_ok=1, hi_ok=1, r1_ok=1, midb_ok=1, mid_ok=1,
            r2_ok=1, low_ok=1, dpre_mm=2, sp_abs=2, sp_exp=2, sp_ln=2, sp_relu=2, delta_ok=2, du_ok=2,
            b_mm=STEPS, c_mm=STEPS, dbu_ok=STEPS, c_ok=STEPS, da_ok=2 * STEPS, h_ok=2 * STEPS,
            hlast_ok=NS, prod=STEPS, pair=STEPS // 2, pair_mm=STEPS // 2, g_ok=NCH,
            x1_mm=1, x1_ok=1, x1g_ok=1,
            q_mm=1, k_mm=1, v_mm=1, q_ok=1, k_ok=1, v_ok=1,
            th_mm=1, ph_mm=1, xt_mm=1, th_ok=1, ph_ok=1, xt_ok=1,
            e_mm=16, nmx=8, nm_ok=16, p_ok=16, turn=32, pt_ok=32, rinv_ok=4, rb_mm=4, rb_ok=4, av_mm=4,
            att_a=4, att_b=2, f_mm=1, f_ok=1, bn_ok=2,
        )
        for name in PER:
            s(name)

        def wait(eng, name, b, k):
            value = b * PER[name] + k
            if isinstance(value, int) and value <= 0:
                return
            eng.wait_ge(S[name], value)

        def at(eng, name, value):
            if isinstance(value, int) and value <= 0:
                return
            eng.wait_ge(S[name], value)

        PARAMS = [
            (w_in_t[:, :], w_in), (w_x_t[:, :, 0:BCR], w_x[:, :, DR:]), (w_x_t[:, :, BCR:2 * BCR], w_x[:, :, DR:]),
            (w_x_t[:, :, 2 * BCR:NROW], w_x[:, :, DR:]), (w_x_t[:, :, NROW:], w_x[:, :, 0:DR]),
            (w_dt_t[NROW:NROW + DR, :], w_dt), (w_out_t[:, :, :], w_out), (w_q_t[:, :], w_q), (w_k_t[:, :], w_k),
            (w_v_t[:, :], w_v), (th_t[:, :], th_w), (ph_t[:, :], ph_w), (cv_t[:, :], cv_w),
            (neg_a[:, :, :], a_log), (taps[:, :, :], conv_w), (w0s[:, :, :], w0),
            (c_b0, b0), (c_lnw, ln_w), (c_lnb, ln_b), (c_bq, b_q), (c_bk, b_k), (c_bv, b_v),
            (c_gam, gam.to_broadcast([128, 1])), (c_bng, bn_g), (c_bnb, bn_b), (c_cb, conv_b), (c_bdt, b_dt), (c_dp, dp),
        ]

        slots = [xin, x0]
        centred = [ta1, ta2]
        turned = [xn[:, 0:CH], xn[:, CH:L]]

        def e_step(m, t):
            return 16 * m + 2 * t + 2 * m

        TAIL = STEPS + 8

        mark = {}

        with nc.Block() as block:

            @block.gpsimd
            def _(pool):
                n = [0]

                def link(ins):
                    n[0] += 1
                    ins.then_inc(S["consts_made"], 1)
                    pool.wait_ge(S["consts_made"], n[0])

                link(pool.memset(ident[:, :], 0.0))
                link(pool.affine_select(out=ident[:, :], in_=ident[:, :], compare_op=ALU.not_equal, fill=1.0,
                                        base=0, pattern=[[-1, 128]], channel_multiplier=1))
                link(pool.memset(mask32[:, :], 0.0))
                for q in range(4):
                    link(pool.affine_select(out=mask32[:, :], in_=mask32[:, :], compare_op=ALU.not_equal, fill=1.0,
                                            base=-32 * q, pattern=[[-1, 32]], channel_multiplier=1))
                link(pool.tensor_copy(sel[:, :, :], mask32[:, :].unsqueeze(2).to_broadcast([128, BCR, 128])))
                link(pool.memset(avg[:, :], 1.0 / C))
                link(pool.tensor_tensor(cent[:, :], ident[:, :], avg[:, :], ALU.subtract))
                link(pool.memset(xi[:, :, 0:KC - 1], 0.0))
                mark["consts"] = n[0]

                def scan_image(b):
                    for h in range(NH):
                        wait(pool, "sp_relu", b, h + 1)
                        wait(pool, "sp_ln", b, h + 1)
                        pool.tensor_tensor(delta[:, h, :], delta[:, h, :], sp_l[h], ALU.add
                                           ).then_inc(S["delta_ok"], 1)
                        wait(pool, "delta_ok", b, h + 1)
                        wait(pool, "xc_ok", b, h + 1)
                        wait(pool, "x1_mm", b - 1, 1)
                        pool.tensor_tensor(du[:, h, :], delta[:, h, :], xc[:, h, :], ALU.mult
                                           ).then_inc(S["du_ok"], 1)
                    for k in range(STEPS):
                        pair, sl = k // 2, k % 2
                        wait(pool, "h_ok", b, 2 * k + 2)
                        wait(pool, "c_ok", b, k + 1)
                        cb = cs[:, sl, :].unsqueeze(1).to_broadcast([128, NH, CH])
                        if k % 2 == 0:
                            wait(pool, "pair_mm", b, pair - 1)
                            pool.tensor_tensor(pa[:, pair % 2, :, :], hs[:, sl, :, :], cb, ALU.mult
                                               ).then_inc(S["prod"], 1)
                        else:
                            wait(pool, "pair", b, pair)
                            pool.tensor_tensor(pc[:, :, :], hs[:, sl, :, :], cb, ALU.mult
                                               ).then_inc(S["prod"], 1)
                        if k < NS:
                            pool.tensor_copy(hlast[:, k, :], hs[:, sl, :, CH - 1]).then_inc(S["hlast_ok"], 1)
                        if k % 2 == 1:
                            wait(pool, "prod", b, k + 1)
                            pool.tensor_tensor(pa[:, pair % 2, :, :], pa[:, pair % 2, :, :], pc[:, :, :], ALU.add
                                               ).then_inc(S["pair"], 1)

                scan_image(0)
                scan_image(1)
                with pool.Fori(2, NB - 1) as b:
                    scan_image(b)
                scan_image(NB - 1)

                def fin(i, k):
                    at(pool, "fscaled", i * 2 + k + 1)
                    pool.tensor_tensor(fbuf[k], fbuf[k], xbuf[k], ALU.add).then_inc(S["fsum"], 1)

                fin(0, 0)
                fin(0, 1)
                with pool.Fori(1, NB // 2) as i:
                    fin(i, 0)
                    fin(i, 1)

            @block.vector
            def _(dve):
                dve.wait_ge(S["weights_in"], 16 * len(PARAMS))
                dve.wait_ge(S["consts_made"], mark["consts"])
                dve.wait_ge(S["mean0"], 2)
                dve.tensor_scalar(c_nshift, c_mean, -1.0 / L, None, ALU.mult).then_inc(S["mean0"], 1)
                n = [0]

                def link(ins, name="stats_chain"):
                    n[0] += 1
                    ins.then_inc(S[name], 1)
                    dve.wait_ge(S[name], n[0])

                dve.wait_ge(S["pe_setup"], 1)
                link(dve.tensor_copy(c_wb, psY[:, 0, 0:4]))
                link(dve.tensor_scalar(w_in_t[:, :], w_in_t[:, :], c_lnw, None, ALU.mult))
                link(dve.tensor_scalar(neg_a[:, :, :], neg_a[:, :, :], -1.0, None, ALU.mult))
                for h in range(NH):
                    link(dve.tensor_scalar(dp_diag[:, h, :], ident[:, :], c_dp[:, h:h + 1], None, ALU.mult))
                link(dve.tensor_tensor(c_gbv, c_gam, c_bv, ALU.mult))
                link(dve.memset(gram[:, :], 0.0))
                link(dve.memset(c_v, EPS_LN))

                def stat(i, k):
                    m = i * 2 + k
                    for q in range(2):
                        at(dve, "st_turned", 2 * m + q + 1)
                        at(dve, "st_gram", m)
                        dve.tensor_copy(turned[q], psT[:, q, :]).then_inc(S["st_copied"], 1)
                    at(dve, "st_gram", m + 1)
                    at(dve, "st_added", m)
                    dve.tensor_tensor(gram[:, :], gram[:, :], psB[:, k, 0:128], ALU.add).then_inc(S["st_added"], 1)

                stat(0, 0)
                stat(0, 1)
                with dve.Fori(1, NB // 2) as i:
                    stat(i, 0)
                    stat(i, 1)
                dve.wait_ge(S["st_added"], NB)
                dve.wait_ge(S["st_centred"], NB)

                for j in range(4):
                    link(dve.tensor_tensor(gram[:, 32 * j:32 * j + 32], gram[:, 32 * j:32 * j + 32], mask32[:, :], ALU.mult))
                    link(dve.reduce_sum(dcov[:, j:j + 1], gram[:, 32 * j:32 * j + 32], AX))
                link(dve.reduce_sum(dcov[:, 4:5], sums[:, :], AX))
                link(dve.tensor_scalar(dcov[:, :], dcov[:, :], 1.0 / (NB * L), None, ALU.mult))
                link(dve.tensor_tensor(c_mean, dcov[:, 4:5], c_nshift, ALU.subtract))
                mark["gathered"] = n[0]
                dve.wait_ge(S["pe_setup"], 2)
                link(dve.tensor_copy(q0[:, 0:20], psT[0:32, 0, 0:20]))

                def cov(i, j):
                    return q0[:, 5 * i + j:5 * i + j + 1]

                def mean(i):
                    return q0[:, 5 * i + 4:5 * i + 5]

                def low(i, j):
                    return q0[:, 20 + 4 * i + j:21 + 4 * i + j]

                def inv(i, j):
                    return q0[:, 36 + 4 * i + j:37 + 4 * i + j]

                def mix(k, i):
                    return q0[:, 52 + 4 * k + i:53 + 4 * k + i]

                tmp, pivot, root = q0[:, 88:89], q0[:, 89:90], q0[:, 90:91]
                for i in range(4):
                    for j in range(i + 1):
                        link(dve.tensor_tensor(tmp, mean(i), mean(j), ALU.mult))
                        link(dve.tensor_tensor(cov(i, j), cov(i, j), tmp, ALU.subtract))
                for j in range(4):
                    link(dve.tensor_scalar(pivot, cov(j, j), EPS0, None, ALU.add))
                    for k in range(j):
                        link(dve.tensor_tensor(tmp, low(j, k), low(j, k), ALU.mult))
                        link(dve.tensor_tensor(pivot, pivot, tmp, ALU.subtract))
                    mark["pivot", j] = n[0]
                    dve.wait_ge(S["stats_act"], j + 1)
                    link(dve.reciprocal(inv(j, j), root))
                    for i in range(j + 1, 4):
                        link(dve.tensor_copy(low(i, j), cov(i, j)))
                        for k in range(j):
                            link(dve.tensor_tensor(tmp, low(i, k), low(j, k), ALU.mult))
                            link(dve.tensor_tensor(low(i, j), low(i, j), tmp, ALU.subtract))
                        link(dve.tensor_tensor(low(i, j), low(i, j), inv(j, j), ALU.mult))
                for j in range(4):
                    for i in range(j + 1, 4):
                        link(dve.tensor_tensor(inv(i, j), low(i, j), inv(j, j), ALU.mult))
                        for k in range(j + 1, i):
                            link(dve.tensor_tensor(tmp, low(i, k), inv(k, j), ALU.mult))
                            link(dve.tensor_tensor(inv(i, j), inv(i, j), tmp, ALU.add))
                        link(dve.scalar_tensor_tensor(out=inv(i, j), in0=inv(i, j), scalar=-1.0, in1=inv(i, i),
                                                      op0=ALU.mult, op1=ALU.mult))
                for k in range(4):
                    for i in range(4):
                        link(dve.tensor_tensor(mix(k, i), w0s[:, i, k:k + 1], inv(k, k), ALU.mult))
                        for j in range(k + 1, 4):
                            link(dve.tensor_tensor(tmp, w0s[:, i, j:j + 1], inv(j, k), ALU.mult))
                            link(dve.tensor_tensor(mix(k, i), mix(k, i), tmp, ALU.add))
                mark["mixed"] = n[0]
                dve.wait_ge(S["pe_setup"], 3)
                link(dve.tensor_copy(wcol[:, :], psT[:, 1, 0:4]))
                for i in range(4):
                    link(dve.tensor_scalar(m0[:, 32 * i:32 * i + 32], mask32[:, :], wcol[:, i:i + 1], None, ALU.mult))
                mark["m0"] = n[0]
                dve.wait_ge(S["pe_setup"], 4)
                link(dve.tensor_tensor(c_c0, c_b0, psY[:, 0, 0:1], ALU.subtract))
                mark["m0_done"] = n[0]

                def front(b):
                    wait(dve, "rs_ok", b, 1)
                    wait(dve, "r2_ok", b - 1, 1)
                    wait(dve, "delta_ok", b - 1, 2)
                    dve.tensor_tensor(xn[:, :], flat(psY), ta1[:, :], ALU.mult).then_inc(S["xn_ok"], 1)
                    c = 0
                    for h in range(NH):
                        wait(dve, "xi_ok", b, h + 1)
                        if h == 0:
                            wait(dve, "pair_mm", b - 1, STEPS // 2)
                        dve.tensor_scalar(xc[:, h, :], xi[:, h, 0:L], taps[:, h, 0:1], c_cb[:, h:h + 1], ALU.mult, ALU.add
                                          ).then_inc(S["conv"], 1)
                        c += 1
                        for t in range(1, KC):
                            wait(dve, "conv", b, c)
                            dve.scalar_tensor_tensor(out=xc[:, h, :], in0=xi[:, h, t:t + L], scalar=taps[:, h, t:t + 1],
                                                     in1=xc[:, h, :], op0=ALU.mult, op1=ALU.add).then_inc(S["conv"], 1)
                            c += 1
                    wait(dve, "dbl_mm", b, 1)
                    dve.tensor_copy(dts[NROW:NROW + DR, :], psE[NROW:NROW + DR, :]).then_inc(S["dt_ok"], 1)
                    wait(dve, "hi_ok", b, 1)
                    dve.tensor_tensor(xn[0:NROW, :], psE[0:NROW, :], bc[0:NROW, :], ALU.subtract).then_inc(S["r1_ok"], 1)
                    wait(dve, "r1_ok", b, 1)
                    dve.tensor_copy(mid[2 * BCR:NROW, :], xn[2 * BCR:NROW, :]).then_inc(S["mid_ok"], 1)
                    wait(dve, "mid_ok", b, 1)
                    dve.tensor_tensor(rem2[2 * BCR:NROW, :], xn[2 * BCR:NROW, :], mid[2 * BCR:NROW, :], ALU.subtract
                                      ).then_inc(S["r2_ok"], 1)
                    wait(dve, "r2_ok", b, 1)
                    dve.tensor_copy(bc[2 * BCR:NROW, :], rem2[2 * BCR:NROW, :]).then_inc(S["low_ok"], 1)

                def step(b, k):
                    ch, n_ = divmod(k, NS)
                    sl = k % 2
                    wait(dve, "b_mm", b, k + 1)
                    if k == 0:
                        wait(dve, "du_ok", b, NH)
                    wait(dve, "h_ok", b, 2 * (k - 1))
                    dve.tensor_tensor(dbu[:, sl, :, :], psB[:, 0, :].unsqueeze(1).to_broadcast([128, NH, CH]),
                                      du[:, :, ch * CH:(ch + 1) * CH], ALU.mult).then_inc(S["dbu_ok"], 1)

                def scans(b, k):
                    ch, n_ = divmod(k, NS)
                    sl = k % 2
                    wait(dve, "prod", b, k - 1)
                    wait(dve, "hlast_ok", b, min(k - 1, NS))
                    if ch:
                        wait(dve, "hlast_ok", b, n_ + 1)
                    wait(dve, "dbu_ok", b, k + 1)
                    for h in range(NH):
                        wait(dve, "da_ok", b, 2 * k + h + 1)
                        dve.tensor_tensor_scan(hs[:, sl, h, :], da[:, sl, h, :], dbu[:, sl, h, :],
                                               hlast[:, n_, h:h + 1] if ch else 0.0, ALU.mult, ALU.add
                                               ).then_inc(S["h_ok"], 1)

                def negmax(a, m, t):
                    i = TILES * m + t
                    wait(dve, "e_mm", a, i + 1)
                    wait(dve, "p_ok", a, i - 1)
                    dve.tensor_reduce(nm[:, i % 2:i % 2 + 1], psE[:, :], AX, ALU.max, negate=True)\
                       .then_inc(S["nmx"] if m else S["nm_ok"], 1)
                    if m:
                        wait(dve, "nmx", a, t + 1)
                        dve.tensor_scalar(nm[:, i % 2:i % 2 + 1], nm[:, i % 2:i % 2 + 1], float(C) ** -0.5, None, ALU.mult
                                          ).then_inc(S["nm_ok"], 1)

                def recips(a, m, gq):
                    i = 2 * m + gq
                    wait(dve, "p_ok", a, 4 * i + 4)
                    wait(dve, "rb_mm", a, i)
                    dve.reciprocal(rinv[:, :], rsum[:, 4 * (i % 2):4 * (i % 2) + 4]).then_inc(S["rinv_ok"], 1)

                def att_out(a, m, gq):
                    i = 2 * m + gq
                    wait(dve, "av_mm", a, i + 1)
                    wait(dve, "rb_ok", a, i + 1)
                    cols = slice(gq * CH, (gq + 1) * CH)
                    if i == 0:
                        at(dve, "f_out", a * 16)
                        at(dve, "x2_out", a * 16)
                    dve.tensor_tensor(fa[:, cols], psT[:, 1, :], rb[:, :], ALU.mult).then_inc(S["att_a"], 1)
                    if m == 0:
                        wait(dve, "att_a", a, i + 1)
                        wait(dve, "x1g_ok", a, 1)
                        dve.scalar_tensor_tensor(out=x2[:, cols], in0=fa[:, cols], scalar=c_gam, in1=x1g[:, cols],
                                                 op0=ALU.mult, op1=ALU.add).then_inc(S["att_b"], 1)

                def image(b, scan, att):
                    a = b - 1
                    if scan:
                        front(b)
                    for k in range(TAIL):
                        if scan and k < STEPS:
                            step(b, k)
                        if att:
                            for m in range(2):
                                for t in range(TILES):
                                    if k == e_step(m, t) + 1:
                                        negmax(a, m, t)
                                for gq in range(2):
                                    if k == e_step(m, 4 * gq + 3) + 2:
                                        recips(a, m, gq)
                                    if k == e_step(m, 4 * gq + 3) + 3:
                                        att_out(a, m, gq)
                        if scan and k < STEPS:
                            scans(b, k)
                        if scan and k in (NS + 2, STEPS):
                            ch = k // NS - 1
                            wait(dve, "pair_mm", b, NS // 2 * (ch + 1))
                            dve.tensor_tensor(g[:, :, ch * CH:(ch + 1) * CH], psY[:, :, :], sz[:, :, ch * CH:(ch + 1) * CH],
                                              ALU.mult).then_inc(S["g_ok"], 1)
                    if scan:
                        wait(dve, "x1_mm", b, 1)
                        dve.tensor_tensor(x1[:, :], psE[:, :], x0[:, :], ALU.add).then_inc(S["x1_ok"], 1)
                    if att:
                        for q in range(2):
                            wait(dve, "f_ok", a, 1)
                            dve.bn_stats(bst[:, bass.ds(a, 1), q, :].rearrange("p a s -> p (a s)"), fa[:, q * CH:(q + 1) * CH]
                                         ).then_inc(S["bn_ok"], 1)

                image(0, True, False)
                image(1, True, True)
                with dve.Fori(2, NB - 1) as b:
                    image(b, True, True)
                image(NB - 1, True, True)
                image(NB, False, True)

                wait(dve, "bn_ok", NB, 0)
                n[0] = 0
                link(dve.bn_aggr(mv[:, :], bst[:, :, :, :].rearrange("p b q s -> p (b q s)")), "fin_chain")
                link(dve.tensor_scalar(c_v2, mv[:, 1:2], EPS_BN, None, ALU.add), "fin_chain")
                dve.wait_ge(S["fin_act"], 1)
                link(dve.reciprocal(c_rs, c_rs), "fin_chain")
                link(dve.tensor_tensor(c_s, c_rs, c_bng, ALU.mult), "fin_chain")
                link(dve.tensor_tensor(c_t, mv[:, 0:1], c_s, ALU.mult), "fin_chain")
                link(dve.tensor_tensor(c_t, c_bnb, c_t, ALU.subtract), "fin_chain")

            @block.scalar
            def _(act):
                act.wait_ge(S["weights_in"], 16 * len(PARAMS))
                act.wait_ge(S["xl0"], 16)
                act.activation(ta1[:, :], xin[:, :], ACT.Copy, accum_out=c_mean).then_inc(S["mean0"], 1)
                act.activation(neg_a[:, :, :], neg_a[:, :, :], ACT.Exp).then_inc(S["mean0"], 1)
                act.wait_ge(S["mean0"], 3)

                def centre(i, k):
                    n = i * 2 + k
                    at(act, f"xl{k}", (i + 1) * 16)
                    at(act, "st_turned", 2 * (n - 1))
                    act.activation(centred[k][:, :], slots[k][:, :], ACT.Identity, bias=c_nshift,
                                   accum_out=sums[:, bass.ds(n, 1)]).then_inc(S["st_centred"], 1)

                centre(0, 0)
                centre(0, 1)
                with act.Fori(1, NB // 2) as i:
                    centre(i, 0)
                    centre(i, 1)

                for j in range(4):
                    act.wait_ge(S["stats_chain"], mark["pivot", j])
                    act.sqrt(q0[:, 90:91], q0[:, 89:90]).then_inc(S["stats_act"], 1)
                act.wait_ge(S["stats_chain"], mark["m0_done"])

                def front(b):
                    act.preload_act_table_set("natural_log_exp_and_others")
                    wait(act, "x0_mm", b, 1)
                    wait(act, "x1_ok", b - 1, 1)
                    act.activation(x0[:, :], psE[:, :], ACT.Identity, bias=c_c0).then_inc(S["x0_ok"], 1)
                    wait(act, "cent_mm", b, 1)
                    act.activation(ta1[:, :], flat(psY), ACT.Square).then_inc(S["sq_ok"], 1)
                    wait(act, "var_mm", b, 1)
                    act.activation(ta2[:, :], psE[:, :], ACT.Ln, bias=c_v).then_inc(S["lnv_ok"], 1)
                    wait(act, "lnv_ok", b, 1)
                    act.activation(ta1[:, :], ta2[:, :], ACT.Exp, scale=-0.5).then_inc(S["rs_ok"], 1)
                    for h, ps in ((0, psY), (1, psB)):
                        wait(act, "xi_mm", b, h + 1)
                        act.activation(xi[:, h, KC - 1:], flat(ps), ACT.Identity, bias=c_wb[:, h:h + 1]
                                       ).then_inc(S["xi_ok"], 1)
                    for h, ps in ((0, psE[:, :]), (1, flat(psT))):
                        wait(act, "z_mm", b, h + 1)
                        act.activation(sz[:, h, :], ps, ACT.Silu, bias=c_wb[:, NH + h:NH + h + 1]
                                       ).then_inc(S["z_ok"], 1)
                    for h in range(NH):
                        wait(act, "conv", b, 4 * h + 4)
                        act.activation(xc[:, h, :], xc[:, h, :], ACT.Silu).then_inc(S["xc_ok"], 1)
                    act.preload_act_table_set("natural_log_exp_and_others")
                    wait(act, "dbl_mm", b, 1)
                    act.activation(bc[0:NROW, :], psE[0:NROW, :], ACT.Copy).then_inc(S["hi_ok"], 1)
                    for h, ps in ((0, psY), (1, psB)):
                        t1, t2 = sp_e[h], sp_l[h]
                        wait(act, "dpre_mm", b, h + 1)
                        act.activation(t1, flat(ps), ACT.Abs, bias=c_bdt[:, h:h + 1]).then_inc(S["sp_abs"], 1)
                        act.activation(delta[:, h, :], flat(ps), ACT.Relu, bias=c_bdt[:, h:h + 1]
                                       ).then_inc(S["sp_relu"], 1)
                        wait(act, "sp_abs", b, h + 1)
                        act.activation(t1, t1, ACT.Exp, scale=-1.0).then_inc(S["sp_exp"], 1)
                        if h == 0:
                            wait(act, "r1_ok", b, 1)
                            act.activation(bc[BCR:2 * BCR, :], xn[BCR:2 * BCR, :], ACT.Copy).then_inc(S["midb_ok"], 1)
                        else:
                            wait(act, "r2_ok", b, 1)
                            wait(act, "midb_ok", b, 1)
                        wait(act, "sp_exp", b, h + 1)
                        act.activation(t2, t1, ACT.Ln, bias=1.0).then_inc(S["sp_ln"], 1)

                def decay(b, k):
                    ch, n = divmod(k, NS)
                    for h in range(NH):
                        if k == 0:
                            wait(act, "delta_ok", b, h + 1)
                        wait(act, "h_ok", b, 2 * (k - 2) + h + 1)
                        act.activation(da[:, k % 2, h, :], delta[:, h, ch * CH:(ch + 1) * CH], ACT.Exp,
                                       scale=neg_a[:, h, n:n + 1]).then_inc(S["da_ok"], 1)

                def c_row(b, k):
                    wait(act, "c_mm", b, k + 1)
                    wait(act, "prod", b, k - 1)
                    act.activation(cs[:, k % 2, :], psB[:, 1, :], ACT.Copy).then_inc(S["c_ok"], 1)

                def numer(a, m, t):
                    i = TILES * m + t
                    wait(act, "nm_ok", a, i + 1)
                    wait(act, "turn", a, 2 * (i - 1))
                    if t % 4 == 0:
                        wait(act, "rinv_ok", a, i // 4 - 1)
                    act.activation(p[:, i % 2, :], psE[:, :], ACT.Exp, bias=nm[:, i % 2:i % 2 + 1],
                                   scale=1.0 if m == 0 else float(C) ** -0.5,
                                   accum_out=rsum[:, i % 8:i % 8 + 1]).then_inc(S["p_ok"], 1)

                def turned_out(a, m, t):
                    i = TILES * m + t
                    for q in range(2):
                        wait(act, "turn", a, 2 * i + q + 1)
                        if t % 4 == 0:
                            wait(act, "av_mm", a, i // 4)
                        act.activation(pt[:, 4 * q:4 * q + 4, 128 * (t % 4):128 * (t % 4) + 128],
                                       psT[:, q, :].rearrange("p (j i) -> p j i", j=4), ACT.Copy
                                       ).then_inc(S["pt_ok"], 1)

                def image(b, scan, att):
                    a = b - 1
                    if scan:
                        front(b)
                    for k in range(TAIL):
                        if scan and k < STEPS:
                            decay(b, k)
                            c_row(b, k)
                        if att:
                            if k == e_step(1, 0) - 1:
                                wait(act, "ph_mm", a, 1)
                                act.activation(ka[0:HD, :], psE[0:HD, :], ACT.Copy).then_inc(S["ph_ok"], 1)
                                wait(act, "th_mm", a, 1)
                                act.activation(qa[0:HD, :], psE[0:HD, :], ACT.Copy).then_inc(S["th_ok"], 1)
                                wait(act, "xt_mm", a, 1)
                                act.activation(va[:, :, :], split(psT), ACT.Copy).then_inc(S["xt_ok"], 1)
                            for m in range(2):
                                for t in range(TILES):
                                    if k == e_step(m, t) + 2:
                                        turned_out(a, m, t)
                                    if k == e_step(m, t) + 1:
                                        numer(a, m, t)
                                for gq in range(2):
                                    if k == e_step(m, 4 * gq + 3) + 2:
                                        wait(act, "rb_mm", a, 2 * m + gq + 1)
                                        wait(act, "att_a", a, 2 * m + gq)
                                        act.activation(rb[:, :], psT[:, 0, :], ACT.Copy).then_inc(S["rb_ok"], 1)
                    if att:
                        wait(act, "f_mm", a, 1)
                        act.activation(fa[:, :], flat(psT), ACT.Copy).then_inc(S["f_ok"], 1)
                    if scan:
                        wait(act, "q_mm", b, 1)
                        act.activation(qa[:, :], psE[:, :], ACT.Identity, bias=c_bq).then_inc(S["q_ok"], 1)
                        wait(act, "k_mm", b, 1)
                        act.activation(ka[:, :], flat(psY), ACT.Identity, bias=c_bk).then_inc(S["k_ok"], 1)
                        wait(act, "x1_ok", b, 1)
                        act.activation(x1g[:, :], x1[:, :], ACT.Identity, bias=c_gbv).then_inc(S["x1g_ok"], 1)
                        wait(act, "v_mm", b, 1)
                        act.activation(va[:, :, :], split(psT), ACT.Copy).then_inc(S["v_ok"], 1)

                image(0, True, False)
                image(1, True, True)
                with act.Fori(2, NB - 1) as b:
                    image(b, True, True)
                image(NB - 1, True, True)
                image(NB, False, True)

                act.wait_ge(S["fin_chain"], 2)
                act.sqrt(c_rs, c_v2).then_inc(S["fin_act"], 1)
                act.wait_ge(S["fin_chain"], 6)

                def fin(i, k):
                    at(act, f"fl{k}", 32 * (i + 1))
                    act.activation(fbuf[k], fbuf[k], ACT.Identity, bias=c_t, scale=c_s).then_inc(S["fscaled"], 1)

                def store(i, k):
                    at(act, "fsum", i * 2 + k + 1)
                    act.dma_start(out[bass.ds(i * 2 + k, 1), :, :].rearrange("a c l -> c (a l)"), fbuf[k]
                                  ).then_inc(S[f"out{k}"], 16)

                def both(i):
                    fin(i, 0)
                    fin(i, 1)
                    store(i, 0)
                    store(i, 1)

                both(0)
                with act.Fori(1, NB // 2) as i:
                    both(i)

            @block.tensor
            def _(pe):
                def mm(dst, lhsT, rhs, start=True, stop=True):
                    return pe.matmul(dst, lhsT, rhs, start=start, stop=stop)

                def wide(dst, lhsT, rhs):
                    for c in range(NCH):
                        last = mm(dst(c), lhsT, rhs[:, c * CH:(c + 1) * CH])
                    return last

                pe.wait_ge(S["weights_in"], 16 * len(PARAMS))
                pe.wait_ge(S["consts_made"], mark["consts"])
                for e in range(4):
                    last = mm(psY[:, 0, e:e + 1], w_in_t[:, 128 * e:128 * e + 128], c_lnb)
                last.then_inc(S["pe_setup"], 1)

                def stat(i, k):
                    m = i * 2 + k
                    at(pe, "st_centred", m + 1)
                    for q in range(2):
                        at(pe, "st_copied", 2 * (m - 1) + q + 1)
                        for j in range(4):
                            last = pe.transpose(psT[:, q, 128 * j:128 * j + 128],
                                                centred[k][:, (4 * q + j) * 128:(4 * q + j + 1) * 128], ident[:, :])
                        last.then_inc(S["st_turned"], 1)
                    at(pe, "st_added", m - 1)
                    for q in range(2):
                        at(pe, "st_copied", 2 * m + q + 1)
                        for j in range(4):
                            blk = turned[q][:, 128 * j:128 * j + 128]
                            last = mm(psB[:, k, 0:128], blk, blk, start=(q == 0 and j == 0), stop=(q == 1 and j == 3))
                    last.then_inc(S["st_gram"], 1)

                stat(0, 0)
                stat(0, 1)
                with pe.Fori(1, NB // 2) as i:
                    stat(i, 0)
                    stat(i, 1)
                pe.wait_ge(S["stats_chain"], mark["gathered"])
                for i in range(4):
                    last = mm(psT[0:32, 0, 5 * i:5 * i + 5], ident[:, 32 * i:32 * i + 32], dcov[:, :])
                last.then_inc(S["pe_setup"], 1)
                pe.wait_ge(S["stats_chain"], mark["mixed"])
                for k in range(4):
                    last = mm(psT[32 * k:32 * k + 32, 1, 0:4], ident[0:32, 0:32], q0[:, 52 + 4 * k:56 + 4 * k])
                last.then_inc(S["pe_setup"], 1)
                pe.wait_ge(S["stats_chain"], mark["m0"])
                mm(psY[:, 0, 0:1], m0[:, :], c_mean).then_inc(S["pe_setup"], 1)
                pe.wait_ge(S["stats_chain"], mark["m0_done"])

                def front(b):
                    at(pe, "x_in", 16 * (b + 1))
                    wait(pe, "q_ok", b - 1, 1)
                    wide(lambda c: psE[:, c * CH:(c + 1) * CH], m0[:, :], xin).then_inc(S["x0_mm"], 1)
                    wait(pe, "x0_ok", b, 1)
                    wait(pe, "k_ok", b - 1, 1)
                    wide(lambda c: psY[:, c, :], cent[:, :], x0).then_inc(S["cent_mm"], 1)
                    wait(pe, "sq_ok", b, 1)
                    wide(lambda c: psE[:, c * CH:(c + 1) * CH], avg[:, :], ta1).then_inc(S["var_mm"], 1)
                    wait(pe, "xn_ok", b, 1)
                    wait(pe, "c_ok", b - 1, STEPS)
                    wait(pe, "v_ok", b - 1, 1)
                    wide(lambda c: psY[:, c, :], w_in_t[:, 0:128], xn).then_inc(S["xi_mm"], 1)
                    wide(lambda c: psB[:, c, :], w_in_t[:, 128:256], xn).then_inc(S["xi_mm"], 1)
                    wide(lambda c: psE[:, c * CH:(c + 1) * CH], w_in_t[:, 256:384], xn).then_inc(S["z_mm"], 1)
                    wide(lambda c: psT[:, c, :], w_in_t[:, 384:512], xn).then_inc(S["z_mm"], 1)
                    wait(pe, "xc_ok", b, NH)
                    for c in range(NCH):
                        for h in range(NH):
                            last = mm(psE[0:NROW + DR, c * CH:(c + 1) * CH], w_x_t[:, h, :],
                                      xc[:, h, c * CH:(c + 1) * CH], start=(h == 0), stop=(h == NH - 1))
                    last.then_inc(S["dbl_mm"], 1)
                    wait(pe, "dt_ok", b, 1)
                    for h, ps in ((0, psY), (1, psB)):
                        for c in range(NCH):
                            last = mm(ps[:, c, :], w_dt_t[NROW:NROW + DR, 128 * h:128 * h + 128],
                                      dts[NROW:NROW + DR, c * CH:(c + 1) * CH])
                        last.then_inc(S["dpre_mm"], 1)

                def rows(b, k):
                    ch, n_ = divmod(k, NS)
                    if k == 0:
                        wait(pe, "low_ok", b, 1)
                        wait(pe, "midb_ok", b, 1)
                        wait(pe, "sp_abs", b, NH)
                        wait(pe, "sp_relu", b, NH)
                    wait(pe, "dbu_ok", b, k)
                    mm(psB[:, 0, :], sel[0:NROW, n_, :], bc[0:NROW, ch * CH:(ch + 1) * CH]).then_inc(S["b_mm"], 1)
                    wait(pe, "c_ok", b, k)
                    mm(psB[:, 1, :], sel[0:NROW, NS + n_, :], bc[0:NROW, ch * CH:(ch + 1) * CH]).then_inc(S["c_mm"], 1)

                def sum_states(b, pr):
                    ch, q = divmod(pr, NS // 2)
                    if q == 0:
                        wait(pe, "g_ok", b, ch)
                        for h in range(NH):
                            mm(psY[:, h, :], dp_diag[:, h, :], xc[:, h, ch * CH:(ch + 1) * CH], stop=False)
                    wait(pe, "pair", b, pr + 1)
                    for h in range(NH):
                        last = mm(psY[:, h, :], ident[:, :], pa[:, pr % 2, h, :], start=False, stop=(q == NS // 2 - 1))
                    last.then_inc(S["pair_mm"], 1)

                def energy(a, m, t):
                    i = TILES * m + t
                    w = C if m == 0 else HD
                    if t == 0:
                        for name in (("q_ok", "k_ok", "v_ok") if m == 0 else ("th_ok", "ph_ok", "xt_ok")):
                            wait(pe, name, a, 1)
                    wait(pe, "p_ok", a, i)
                    for c in range(NCH):
                        last = mm(psE[:, c * CH:(c + 1) * CH], qa[0:w, 128 * t:128 * t + 128], ka[0:w, c * CH:(c + 1) * CH])
                    last.then_inc(S["e_mm"], 1)

                def turn(a, m, t):
                    i = TILES * m + t
                    wait(pe, "p_ok", a, i + 1)
                    for q in range(2):
                        wait(pe, "pt_ok", a, 2 * (i - 1) + q + 1)
                        if t % 4 == 0 and i:
                            if q == 0:
                                wait(pe, "rb_ok", a, i // 4)
                            else:
                                wait(pe, "att_a", a, i // 4)
                        for j in range(4):
                            last = pe.transpose(psT[:, q, 128 * j:128 * j + 128],
                                                p[:, i % 2, (4 * q + j) * 128:(4 * q + j + 1) * 128], ident[:, :])
                        last.then_inc(S["turn"], 1)

                def values(a, m, gq):
                    i = 2 * m + gq
                    wait(pe, "rinv_ok", a, i + 1)
                    wait(pe, "pt_ok", a, 8 * i + 8)
                    for t in range(4):
                        last = mm(psT[:, 0, 128 * t:128 * t + 128], rinv[:, t:t + 1].to_broadcast([128, 128]), ident[:, :])
                    last.then_inc(S["rb_mm"], 1)
                    for j in range(TB):
                        last = mm(psT[:, 1, :], va[:, j, :], pt[:, j, :], start=(j == 0), stop=(j == TB - 1))
                    last.then_inc(S["av_mm"], 1)

                def image(b, scan, att):
                    a = b - 1
                    if scan:
                        front(b)
                    for k in range(TAIL):
                        if scan and k < STEPS:
                            rows(b, k)
                        if att:
                            if k == e_step(1, 0) - 1:
                                wait(pe, "att_b", a, 2)
                                wait(pe, "p_ok", a, TILES)
                                wide(lambda c: psE[0:HD, c * CH:(c + 1) * CH], ph_t[:, :], x2).then_inc(S["ph_mm"], 1)
                                wait(pe, "ph_ok", a, 1)
                                wide(lambda c: psE[0:HD, c * CH:(c + 1) * CH], th_t[:, :], x2).then_inc(S["th_mm"], 1)
                                wait(pe, "pt_ok", a, 2 * TILES)
                                wait(pe, "rb_ok", a, 2)
                                for j in range(TB):
                                    last = pe.transpose(split(psT)[:, j, :], x2[:, 128 * j:128 * j + 128], ident[:, :])
                                last.then_inc(S["xt_mm"], 1)
                            for m in range(2):
                                for t in range(TILES):
                                    if k == e_step(m, t) + 2:
                                        turn(a, m, t)
                                        if t % 4 == 3:
                                            values(a, m, t // 4)
                                for t in range(TILES):
                                    if k == e_step(m, t):
                                        energy(a, m, t)
                        if scan and k % 2 == 1 and 3 <= k <= STEPS + 1:
                            sum_states(b, (k - 3) // 2)
                    if scan:
                        wait(pe, "g_ok", b, NCH)
                        if att:
                            wait(pe, "p_ok", a, 2 * TILES)
                        for c in range(NCH):
                            for h in range(NH):
                                last = mm(psE[:, c * CH:(c + 1) * CH], w_out_t[:, h, :], g[:, h, c * CH:(c + 1) * CH],
                                          start=(h == 0), stop=(h == NH - 1))
                        last.then_inc(S["x1_mm"], 1)
                    if att:
                        wait(pe, "att_a", a, 4)
                        wait(pe, "pt_ok", a, 4 * TILES)
                        wide(lambda c: psT[:, c, :], cv_t[:, :], fa).then_inc(S["f_mm"], 1)
                    if scan:
                        wait(pe, "x1_ok", b, 1)
                        wide(lambda c: psE[:, c * CH:(c + 1) * CH], w_q_t[:, :], x1).then_inc(S["q_mm"], 1)
                        wide(lambda c: psY[:, c, :], w_k_t[:, :], x1).then_inc(S["k_mm"], 1)
                        if att:
                            wait(pe, "f_ok", a, 1)
                        for j in range(TB):
                            last = mm(split(psT)[:, j, :], x1[:, 128 * j:128 * j + 128], w_v_t[:, :])
                        last.then_inc(S["v_mm"], 1)

                image(0, True, False)
                image(1, True, True)
                with pe.Fori(2, NB - 1) as b:
                    image(b, True, True)
                image(NB - 1, True, True)
                image(NB, False, True)

            @block.sync
            def _(sp):
                for dst, src in PARAMS:
                    sp.dma_start(dst, src).then_inc(S["weights_in"], 16)

                def load_stat(i, k):
                    at(sp, "st_centred", i * 2 + k - 1)
                    sp.dma_start(slots[k][:, :], x[bass.ds(i * 2 + k, 1), :, :].rearrange("a c l -> c (a l)")
                                 ).then_inc(S[f"xl{k}"], 16)

                load_stat(0, 0)
                load_stat(0, 1)
                with sp.Fori(1, NB // 2) as i:
                    load_stat(i, 0)
                    load_stat(i, 1)
                at(sp, "st_centred", NB)
                sp.dma_start(xin[:, :], x[0, :, :]).then_inc(S["x_in"], 16)

                def image(b, scan, att):
                    if scan and not (isinstance(b, int) and b == NB - 1):
                        wait(sp, "x0_mm", b, 1)
                        sp.dma_start(xin[:, :], x[bass.ds(b + 1, 1), :, :].rearrange("a c l -> c (a l)")
                                     ).then_inc(S["x_in"], 16)
                    if att:
                        a = b - 1
                        wait(sp, "att_b", a, 2)
                        sp.dma_start(x2_dram[bass.ds(a, 1), :, :].rearrange("a c l -> c (a l)"), x2[:, :]
                                     ).then_inc(S["x2_out"], 16)
                        wait(sp, "f_ok", a, 1)
                        sp.dma_start(f_dram[bass.ds(a, 1), :, :].rearrange("a c l -> c (a l)"), fa[:, :]
                                     ).then_inc(S["f_out"], 16)

                image(0, True, False)
                image(1, True, True)
                with sp.Fori(2, NB - 1) as b:
                    image(b, True, True)
                image(NB - 1, True, True)
                image(NB, False, True)

                at(sp, "f_out", 16 * NB)
                at(sp, "x2_out", 16 * NB)
                at(sp, "fin_chain", 6)

                def load_fin(i, k):
                    at(sp, f"out{k}", 16 * i)
                    n = i * 2 + k
                    sp.dma_start(fbuf[k], f_dram[bass.ds(n, 1), :, :].rearrange("a c l -> c (a l)")
                                 ).then_inc(S[f"fl{k}"], 16)
                    sp.dma_start(xbuf[k], x2_dram[bass.ds(n, 1), :, :].rearrange("a c l -> c (a l)")
                                 ).then_inc(S[f"fl{k}"], 16)

                load_fin(0, 0)
                load_fin(0, 1)
                with sp.Fori(1, NB // 2) as i:
                    load_fin(i, 0)
                    load_fin(i, 1)
                at(sp, "out0", 16 * (NB // 2))
                at(sp, "out1", 16 * (NB // 2))


def kernel(x, L0_conv_weight, L0_conv_bias, L1_conv_ln_w, L1_conv_ln_b, L1_conv_W_in, L1_conv_conv_w, L1_conv_conv_b,
           L1_conv_W_x, L1_conv_W_dt, L1_conv_b_dt, L1_conv_A_log, L1_conv_Dp, L1_conv_W_out, L2_conv_Wq, L2_conv_bq,
           L2_conv_Wk, L2_conv_bk, L2_conv_Wv, L2_conv_bv, L2_conv_gamma, L3_conv_theta_w, L3_conv_phi_w, L3_conv_conv_w,
           L3_conv_gamma, L3_conv_beta):
    import numpy as np
    import concourse.bacc as bacc
    from concourse.bass_utils import run_bass_kernel_spmd

    def col(v):
        return np.asarray(v).reshape(C, 1)

    def halves(v):
        v = np.asarray(v).reshape(NH, C, -1).transpose(1, 0, 2)
        return v

    arrays = dict(
        x=np.asarray(x).reshape(NB, C, L),
        w0=np.asarray(L0_conv_weight).transpose(2, 0, 1), b0=col(L0_conv_bias), ln_w=col(L1_conv_ln_w), ln_b=col(L1_conv_ln_b),
        w_in=np.asarray(L1_conv_W_in).T, conv_w=halves(L1_conv_conv_w), conv_b=halves(L1_conv_conv_b)[:, :, 0],
        w_x=halves(np.asarray(L1_conv_W_x).T), w_dt=np.asarray(L1_conv_W_dt).T, b_dt=halves(L1_conv_b_dt)[:, :, 0],
        a_log=halves(L1_conv_A_log), dp=halves(L1_conv_Dp)[:, :, 0], w_out=halves(np.asarray(L1_conv_W_out).T),
        w_q=np.asarray(L2_conv_Wq).T, b_q=col(L2_conv_bq), w_k=np.asarray(L2_conv_Wk).T, b_k=col(L2_conv_bk),
        w_v=np.asarray(L2_conv_Wv).T, b_v=col(L2_conv_bv), gam=np.asarray(L2_conv_gamma).reshape(1, 1),
        th_w=np.asarray(L3_conv_theta_w).T, ph_w=np.asarray(L3_conv_phi_w).T, cv_w=np.asarray(L3_conv_conv_w).T,
        bn_g=col(L3_conv_gamma), bn_b=col(L3_conv_beta),
    )
    arrays = {k: np.ascontiguousarray(v) for k, v in arrays.items()}
    nc = bacc.Bacc("TRN2", target_bir_lowering=False, num_devices=1)
    aps = {k: nc.dram_tensor(k, v.shape, mybir.dt.from_np(v.dtype), kind="ExternalInput").ap() for k, v in arrays.items()}
    out = nc.dram_tensor("out", (NB, C, L), mybir.dt.float32, kind="ExternalOutput").ap()
    build(nc, out=out, **aps)
    result = run_bass_kernel_spmd(nc, [arrays], core_ids=[0])
    return result.results[0]["out"].reshape(NB, C, HH, WW)
```

```python
from contextlib import ExitStack

import concourse.bass as bass
from concourse import mybir

NB, C, HH, WW = 32, 128, 32, 32
L = HH * WW
F = C // 4
DI = 2 * C
NH = DI // C
NS = 16
KC = 4
DR = C // 16
CH = 512
NCH = L // CH
BCR = 2 * NS
NROW = 3 * BCR
TB = L // 128
HD = C // 2
STEPS = NCH * NS
TILES = TB
GT = 2
NG = 2 * TILES // GT
GL = GT * 128
EPS0, EPS_LN, EPS_BN = 1e-5, 1e-5, 1e-5


def build(nc, x, w0, b0, ln_w, ln_b, w_in, conv_w, conv_b, w_x, w_dt, b_dt, a_log, dp, w_out,
          w_q, b_q, w_k, b_k, w_v, b_v, gam, th_w, ph_w, cv_w, bn_g, bn_b, out):
    fp32, bf16 = mybir.dt.float32, mybir.dt.bfloat16
    ALU = mybir.AluOpType
    ACT = mybir.ActivationFunctionType
    AX = mybir.AxisListType.X
    ctx = ExitStack()
    with ctx:
        def sb(name, shape, dt=fp32):
            return ctx.enter_context(nc.sbuf_tensor(name, shape, dt))

        def pb(name, shape):
            return ctx.enter_context(nc.psum_tensor(name, shape, fp32))

        def sem(name):
            return ctx.enter_context(nc.semaphore(name))

        x2_dram = nc.dram_tensor("x2_scratch", [NB, C, L], fp32).ap()
        f_dram = nc.dram_tensor("f_scratch", [NB, C, L], fp32).ap()

        ident = sb("ident", [128, 128])
        mask32 = sb("mask32", [128, 32])
        sel = sb("sel", [128, BCR, 128], bf16)
        cent = sb("cent", [128, 128])
        avg = sb("avg", [128, 128])
        m0 = sb("m0", [128, 128])
        m0_rows = sb("m0_rows", [128, 128])
        m0c = sb("m0c", [128, 128])
        w_in_t = sb("w_in_t", [128, 2 * DI])
        w_x_t = sb("w_x_t", [128, NH, NROW + DR])
        w_dt_t = sb("w_dt_t", [128, DI])
        w_out_t = sb("w_out_t", [128, NH, C])
        w_q_t = sb("w_q_t", [128, C])
        w_k_t = sb("w_k_t", [128, C])
        w_v_t = sb("w_v_t", [128, C])
        th_t = sb("th_t", [128, HD])
        ph_t = sb("ph_t", [128, HD])
        cv_t = sb("cv_t", [128, C])
        dp_diag = sb("dp_diag", [128, NH, 128])
        cvec = sb("cvec", [128, 32])
        neg_a = sb("neg_a", [128, NH, NS])
        taps = sb("taps", [128, NH, KC])
        (c_b0, c_lnw, c_lnb, c_bq, c_bk, c_bv, c_gam, c_bng, c_bnb, c_c0, c_nshift, c_mean, c_gbv,
         c_s, c_t, c_v, c_rs, c_v2, c_cc, c_c0g) = (cvec[:, i:i + 1] for i in range(20))
        c_cb, c_bdt, c_dp = (cvec[:, 20 + 2 * i:22 + 2 * i] for i in range(3))
        c_wb = cvec[:, 26:30]

        sums = sb("sums", [128, NB])
        gram = sb("gram", [128, 128])
        dcov = sb("dcov", [128, 5])
        q0 = sb("q0", [32, 96])
        w0s = sb("w0s", [32, 4, 4])
        wcol = sb("wcol", [128, 4])

        xin = sb("xin", [128, L])
        xres = sb("xres", [128, L])
        xcen = sb("xcen", [128, CH])
        sq = sb("sq", [128, CH])
        lnv = sb("lnv", [128, CH])
        rstd = sb("rstd", [128, CH])
        xn = sb("xn", [128, CH])
        xi = sb("xi", [128, NH, KC - 1 + L])
        xc = sb("xc", [128, NH, L])
        sz = sb("sz", [128, NH, L])
        sp_e = sb("sp_e", [128, NH, CH])
        sp_l = sb("sp_l", [128, NH, CH])
        rem = sb("rem", [128, 2, CH])
        dts = sb("dts", [128, CH])
        delta = sb("delta", [128, NH, L])
        du = sb("du", [128, NH, L])
        bc = sb("bc", [128, L], bf16)
        mid = sb("mid", [128, CH], bf16)
        da = sb("da", [128, 2, NH, CH])
        dbu = sb("dbu", [128, 2, NH, CH])
        hs = sb("hs", [128, 2, NH, CH])
        hlast = sb("hlast", [128, NS, NH])
        cs = sb("cs", [128, 2, CH])
        pa = sb("pa", [128, 2, NH, CH])
        pc = sb("pc", [128, NH, CH])
        x1 = sb("x1", [128, L])
        x1g = sb("x1g", [128, L])
        qa = sb("qa", [128, L])
        ka = sb("ka", [128, L])
        va = sb("va", [128, TB, C])
        p = sb("p", [128, 2, L])
        pt = sb("pt", [128, 2, TB, GL])
        fa = sb("fa", [128, L])
        x2 = sb("x2", [128, L])
        nm = sb("nm", [128, 2])
        rsum = sb("rsum", [128, 2])
        rinv = sb("rinv", [128, 2])
        bst = sb("bst", [128, NB, NG // 2, 6])
        mv = sb("mv", [128, 2])
        g = du
        fbuf = [t[:, :, :] for t in (delta, xc)] + [t[:, :, :, :].rearrange("p a h n -> p a (h n)") for t in (hs, da)]
        xbuf = [t[:, :, :] for t in (du, sz)] + [t[:, :, :, :].rearrange("p a h n -> p a (h n)") for t in (pa, dbu)]
        SLOTS = len(fbuf)
        ROUNDS = NB // (2 * SLOTS)

        psE = pb("psE", [128, 2, CH])
        psY = pb("psY", [128, NH, CH])
        psR = pb("psR", [128, CH])
        psT = pb("psT", [128, 2, CH])
        psA = pb("psA", [128, CH])

        def flat(t):
            return t[:, :, :].rearrange("p a n -> p (a n)")

        def split(t):
            return flat(t).rearrange("p (j n) -> p j n", j=TB)

        S = {}

        def s(name):
            if name not in S:
                S[name] = sem(name)
            return S[name]

        for name in ("weights_in", "consts_made", "setup_chain", "mean0", "stats_chain", "stats_act",
                     "xl0", "xl1", "st_centred", "st_turned", "st_copied", "st_gram", "st_added",
                     "x_in", "xr_in0", "xr_in1", "x2_out", "f_out", "fin_chain", "fin_act", "pe_setup",
                     "fscaled", "fsum"):
            s(name)
        for k in range(SLOTS):
            s(f"fl{k}")
            s(f"out{k}")

        PER = dict(
            cent_mm=NCH, xcen_ok=NCH, sq_ok=NCH, var_mm=NCH, lnv_ok=NCH, rs_ok=NCH, xn_ok=NCH,
            xi_mm=2 * NCH, xi_ok=2 * NCH, conv=8 * NCH, z_mm=2 * NCH, z_ok=2 * NCH, xc_ok=2 * NCH,
            dbl_mm=NCH, dt_ok=NCH, hi_ok=NCH, r1_ok=NCH, midb_ok=NCH, mid_ok=NCH, r2_ok=NCH, low_ok=NCH,
            dpre_mm=2 * NCH, sp_abs=2 * NCH, sp_relu=2 * NCH, sp_exp=2 * NCH, sp_ln=2 * NCH,
            delta_ok=2 * NCH, du_ok=2 * NCH,
            b_mm=STEPS, c_mm=STEPS, dbu_ok=STEPS, c_ok=STEPS, da_ok=2 * STEPS, h_ok=2 * STEPS,
            hlast_ok=NS, prod=STEPS, pair=STEPS // 2, pair_mm=STEPS // 2, g_ok=NCH,
            x1_mm=NCH, x1_ok=NCH, x1g_ok=NCH,
            q_mm=2, k_mm=2, v_mm=2, q_ok=2, k_ok=2, v_ok=2,
            e_mm=16, nm_ok=16, p_ok=16, turn=32, pt_ok=32, rinv_ok=16, pn_ok=16, av_mm=NG,
            out_ok=NG, bn_ok=NG // 2,
        )
        for name in PER:
            s(name)

        def wait(eng, name, b, k):
            value = b * PER[name] + k
            if isinstance(value, int) and value <= 0:
                return
            eng.wait_ge(S[name], value)

        def at(eng, name, value):
            if isinstance(value, int) and value <= 0:
                return
            eng.wait_ge(S[name], value)

        PARAMS = [
            (w_in_t[:, :], w_in), (w_x_t[:, :, 0:BCR], w_x[:, :, DR:]), (w_x_t[:, :, BCR:2 * BCR], w_x[:, :, DR:]),
            (w_x_t[:, :, 2 * BCR:NROW], w_x[:, :, DR:]), (w_x_t[:, :, NROW:], w_x[:, :, 0:DR]),
            (w_dt_t[NROW:NROW + DR, :], w_dt), (w_out_t[:, :, :], w_out), (w_q_t[:, :], w_q), (w_k_t[:, :], w_k),
            (w_v_t[:, :], w_v), (th_t[:, :], th_w), (ph_t[:, :], ph_w), (cv_t[:, :], cv_w),
            (neg_a[:, :, :], a_log), (taps[:, :, :], conv_w), (w0s[:, :, :], w0),
            (c_b0, b0), (c_lnw, ln_w), (c_lnb, ln_b), (c_bq, b_q), (c_bk, b_k), (c_bv, b_v),
            (c_gam, gam.to_broadcast([128, 1])), (c_bng, bn_g), (c_bnb, bn_b), (c_cb, conv_b), (c_bdt, b_dt), (c_dp, dp),
        ]

        slots = [xin, xres]
        centred = [x1, x2]
        turned = [qa[:, 0:CH], qa[:, CH:L]]

        TILE_AT = [6, 7, 11, 12, 13, 14, 15, 16]
        TILE_STEP = {16 * m + TILE_AT[t]: (m, t) for m in range(2) for t in range(TILES)}
        LATE = 4
        AT_C, AT_X, AT_Z, AT_P = 2, 5, 9, 11
        AT_R, AT_Q, AT_V = 3, 4, 6
        AT_DX = 8

        def cols(c):
            return slice(c * CH, (c + 1) * CH)

        mark = {}

        with nc.Block() as block:

            @block.gpsimd
            def _(pool):
                n = [0]

                def link(ins):
                    n[0] += 1
                    ins.then_inc(S["consts_made"], 1)
                    pool.wait_ge(S["consts_made"], n[0])

                link(pool.memset(ident[:, :], 0.0))
                link(pool.affine_select(out=ident[:, :], in_=ident[:, :], compare_op=ALU.not_equal, fill=1.0,
                                        base=0, pattern=[[-1, 128]], channel_multiplier=1))
                link(pool.memset(mask32[:, :], 0.0))
                for q in range(4):
                    link(pool.affine_select(out=mask32[:, :], in_=mask32[:, :], compare_op=ALU.not_equal, fill=1.0,
                                            base=-32 * q, pattern=[[-1, 32]], channel_multiplier=1))
                link(pool.tensor_copy(sel[:, :, :], mask32[:, :].unsqueeze(2).to_broadcast([128, BCR, 128])))
                link(pool.memset(avg[:, :], 1.0 / C))
                link(pool.tensor_tensor(cent[:, :], ident[:, :], avg[:, :], ALU.subtract))
                link(pool.memset(xi[:, :, 0:KC - 1], 0.0))
                mark["consts"] = n[0]

                def front(fb, fc, r):
                    h = {AT_P + 2: 0, AT_P + 3: 1}.get(r)
                    if h is not None:
                        i = 2 * fc + h + 1
                        wait(pool, "sp_relu", fb, i)
                        wait(pool, "sp_ln", fb, i)
                        pool.tensor_tensor(delta[:, h, cols(fc)], delta[:, h, cols(fc)], sp_l[:, h, :], ALU.add
                                           ).then_inc(S["delta_ok"], 1)
                        wait(pool, "delta_ok", fb, i)
                        wait(pool, "xc_ok", fb, i)
                        wait(pool, "x1_mm", fb - 1, fc + 1)
                        pool.tensor_tensor(du[:, h, cols(fc)], delta[:, h, cols(fc)], xc[:, h, cols(fc)], ALU.mult
                                           ).then_inc(S["du_ok"], 1)

                def products(b, k):
                    pair, sl = k // 2, k % 2
                    wait(pool, "h_ok", b, 2 * k + 2)
                    wait(pool, "c_ok", b, k + 1)
                    c_all = cs[:, sl, :].unsqueeze(1).to_broadcast([128, NH, CH])
                    if k % 2 == 0:
                        wait(pool, "pair_mm", b, pair - 1)
                        pool.tensor_tensor(pa[:, pair % 2, :, :], hs[:, sl, :, :], c_all, ALU.mult
                                           ).then_inc(S["prod"], 1)
                    else:
                        wait(pool, "pair", b, pair)
                        pool.tensor_tensor(pc[:, :, :], hs[:, sl, :, :], c_all, ALU.mult
                                           ).then_inc(S["prod"], 1)
                    if k < NS:
                        pool.tensor_copy(hlast[:, k, :], hs[:, sl, :, CH - 1]).then_inc(S["hlast_ok"], 1)
                    if k % 2 == 1:
                        wait(pool, "prod", b, k + 1)
                        pool.tensor_tensor(pa[:, pair % 2, :, :], pa[:, pair % 2, :, :], pc[:, :, :], ALU.add
                                           ).then_inc(S["pair"], 1)

                def image(b, scan, more):
                    for c in range(NCH):
                        for r in range(NS):
                            if c == 0 and scan:
                                front(b, 1, r)
                            if c == 1 and more:
                                front(b + 1, 0, r)
                            if scan:
                                products(b, NS * c + r)

                for r in range(NS):
                    front(0, 0, r)
                image(0, True, True)
                image(1, True, True)
                with pool.Fori(2, NB - 1) as b:
                    image(b, True, True)
                image(NB - 1, True, False)

            @block.vector
            def _(dve):
                dve.wait_ge(S["weights_in"], 16 * len(PARAMS))
                dve.wait_ge(S["consts_made"], mark["consts"])
                dve.wait_ge(S["mean0"], 2)
                dve.tensor_scalar(c_nshift, c_mean, -1.0 / L, None, ALU.mult).then_inc(S["mean0"], 1)
                n = [0]

                def link(ins, name="stats_chain"):
                    n[0] += 1
                    ins.then_inc(S[name], 1)
                    dve.wait_ge(S[name], n[0])

                dve.wait_ge(S["pe_setup"], 1)
                link(dve.tensor_copy(c_wb, psY[:, 0, 0:4]))
                link(dve.tensor_scalar(w_in_t[:, :], w_in_t[:, :], c_lnw, None, ALU.mult))
                link(dve.tensor_scalar(neg_a[:, :, :], neg_a[:, :, :], -1.0, None, ALU.mult))
                for h in range(NH):
                    link(dve.tensor_scalar(dp_diag[:, h, :], ident[:, :], c_dp[:, h:h + 1], None, ALU.mult))
                link(dve.tensor_tensor(c_gbv, c_gam, c_bv, ALU.mult))
                link(dve.memset(gram[:, :], 0.0))
                link(dve.memset(c_v, EPS_LN))

                def stat(i, k):
                    m = i * 2 + k
                    for q in range(2):
                        at(dve, "st_turned", 2 * m + q + 1)
                        at(dve, "st_gram", m)
                        dve.tensor_copy(turned[q], psT[:, q, :]).then_inc(S["st_copied"], 1)
                    at(dve, "st_gram", m + 1)
                    at(dve, "st_added", m)
                    dve.tensor_tensor(gram[:, :], gram[:, :], (psR[:, 0:128], psY[:, 1, 0:128])[k], ALU.add).then_inc(S["st_added"], 1)

                stat(0, 0)
                stat(0, 1)
                with dve.Fori(1, NB // 2) as i:
                    stat(i, 0)
                    stat(i, 1)
                dve.wait_ge(S["st_added"], NB)
                dve.wait_ge(S["st_centred"], NB)

                for j in range(4):
                    link(dve.tensor_tensor(gram[:, 32 * j:32 * j + 32], gram[:, 32 * j:32 * j + 32], mask32[:, :], ALU.mult))
                    link(dve.reduce_sum(dcov[:, j:j + 1], gram[:, 32 * j:32 * j + 32], AX))
                link(dve.reduce_sum(dcov[:, 4:5], sums[:, :], AX))
                link(dve.tensor_scalar(dcov[:, :], dcov[:, :], 1.0 / (NB * L), None, ALU.mult))
                link(dve.tensor_tensor(c_mean, dcov[:, 4:5], c_nshift, ALU.subtract))
                mark["gathered"] = n[0]
                dve.wait_ge(S["pe_setup"], 2)
                link(dve.tensor_copy(q0[:, 0:20], psT[0:32, 0, 0:20]))

                def cov(i, j):
                    return q0[:, 5 * i + j:5 * i + j + 1]

                def mean(i):
                    return q0[:, 5 * i + 4:5 * i + 5]

                def low(i, j):
                    return q0[:, 20 + 4 * i + j:21 + 4 * i + j]

                def inv(i, j):
                    return q0[:, 36 + 4 * i + j:37 + 4 * i + j]

                def mix(k, i):
                    return q0[:, 52 + 4 * k + i:53 + 4 * k + i]

                tmp, pivot, root = q0[:, 88:89], q0[:, 89:90], q0[:, 90:91]
                for i in range(4):
                    for j in range(i + 1):
                        link(dve.tensor_tensor(tmp, mean(i), mean(j), ALU.mult))
                        link(dve.tensor_tensor(cov(i, j), cov(i, j), tmp, ALU.subtract))
                for j in range(4):
                    link(dve.tensor_scalar(pivot, cov(j, j), EPS0, None, ALU.add))
                    for k in range(j):
                        link(dve.tensor_tensor(tmp, low(j, k), low(j, k), ALU.mult))
                        link(dve.tensor_tensor(pivot, pivot, tmp, ALU.subtract))
                    mark["pivot", j] = n[0]
                    dve.wait_ge(S["stats_act"], j + 1)
                    link(dve.reciprocal(inv(j, j), root))
                    for i in range(j + 1, 4):
                        link(dve.tensor_copy(low(i, j), cov(i, j)))
                        for k in range(j):
                            link(dve.tensor_tensor(tmp, low(i, k), low(j, k), ALU.mult))
                            link(dve.tensor_tensor(low(i, j), low(i, j), tmp, ALU.subtract))
                        link(dve.tensor_tensor(low(i, j), low(i, j), inv(j, j), ALU.mult))
                for j in range(4):
                    for i in range(j + 1, 4):
                        link(dve.tensor_tensor(inv(i, j), low(i, j), inv(j, j), ALU.mult))
                        for k in range(j + 1, i):
                            link(dve.tensor_tensor(tmp, low(i, k), inv(k, j), ALU.mult))
                            link(dve.tensor_tensor(inv(i, j), inv(i, j), tmp, ALU.add))
                        link(dve.scalar_tensor_tensor(out=inv(i, j), in0=inv(i, j), scalar=-1.0, in1=inv(i, i),
                                                      op0=ALU.mult, op1=ALU.mult))
                for k in range(4):
                    for i in range(4):
                        link(dve.tensor_tensor(mix(k, i), w0s[:, i, k:k + 1], inv(k, k), ALU.mult))
                        for j in range(k + 1, 4):
                            link(dve.tensor_tensor(tmp, w0s[:, i, j:j + 1], inv(j, k), ALU.mult))
                            link(dve.tensor_tensor(mix(k, i), mix(k, i), tmp, ALU.add))
                mark["mixed"] = n[0]
                dve.wait_ge(S["pe_setup"], 3)
                link(dve.tensor_copy(wcol[:, :], psT[:, 1, 0:4]))
                for i in range(4):
                    link(dve.tensor_scalar(m0[:, 32 * i:32 * i + 32], mask32[:, :], wcol[:, i:i + 1], None, ALU.mult))
                mark["m0"] = n[0]
                dve.wait_ge(S["pe_setup"], 4)
                link(dve.tensor_tensor(c_c0, c_b0, psY[:, 0, 0:1], ALU.subtract))
                link(dve.tensor_tensor(c_c0g, c_c0, c_gbv, ALU.add))
                link(dve.tensor_copy(m0_rows[:, :], psY[:, 1, 0:128]))
                mark["m0_rows"] = n[0]
                dve.wait_ge(S["pe_setup"], 5)
                link(dve.tensor_copy(m0c[:, :], psT[:, 0, 0:128]))
                link(dve.tensor_copy(c_cc, psT[:, 1, 0:1]))
                mark["m0_done"] = n[0]

                def front(fb, fc, r):
                    if r == AT_C + 2:
                        wait(dve, "rs_ok", fb, fc + 1)
                        wait(dve, "xcen_ok", fb, fc + 1)
                        dve.tensor_tensor(xn[:, :], xcen[:, :], rstd[:, :], ALU.mult).then_inc(S["xn_ok"], 1)
                    for h, t in {AT_X + 1: [(0, 0), (0, 1)], AT_X + 2: [(0, 2), (0, 3)],
                                 AT_X + 3: [(1, 0), (1, 1)], AT_X + 4: [(1, 2), (1, 3)]}.get(r, []):
                        i = 2 * fc + h
                        src = xi[:, h, fc * CH + t:fc * CH + t + CH]
                        if t == 0:
                            wait(dve, "xi_ok", fb, i + 1)
                            wait(dve, "pair_mm", fb - 1, NS // 2 * fc + AT_DX // 2)
                            dve.tensor_scalar(xc[:, h, cols(fc)], src, taps[:, h, 0:1], c_cb[:, h:h + 1],
                                              ALU.mult, ALU.add).then_inc(S["conv"], 1)
                        else:
                            wait(dve, "conv", fb, 4 * i + t)
                            dve.scalar_tensor_tensor(out=xc[:, h, cols(fc)], in0=src,
                                                     scalar=taps[:, h, t:t + 1], in1=xc[:, h, cols(fc)],
                                                     op0=ALU.mult, op1=ALU.add).then_inc(S["conv"], 1)
                    if r == AT_Z + 1:
                        wait(dve, "dbl_mm", fb, fc + 1)
                        dve.tensor_copy(dts[NROW:NROW + DR, :], psE[NROW:NROW + DR, 0, :]).then_inc(S["dt_ok"], 1)
                        wait(dve, "hi_ok", fb, fc + 1)
                        dve.tensor_tensor(rem[0:NROW, 0, :], psE[0:NROW, 0, :], bc[0:NROW, cols(fc)], ALU.subtract
                                          ).then_inc(S["r1_ok"], 1)
                    if r == AT_Z + 2:
                        wait(dve, "r1_ok", fb, fc + 1)
                        dve.tensor_copy(mid[2 * BCR:NROW, :], rem[2 * BCR:NROW, 0, :]).then_inc(S["mid_ok"], 1)
                    if r == AT_Z + 3:
                        wait(dve, "mid_ok", fb, fc + 1)
                        dve.tensor_tensor(rem[2 * BCR:NROW, 1, :], rem[2 * BCR:NROW, 0, :], mid[2 * BCR:NROW, :],
                                          ALU.subtract).then_inc(S["r2_ok"], 1)
                    if r == AT_Z + 4:
                        wait(dve, "r2_ok", fb, fc + 1)
                        dve.tensor_copy(bc[2 * BCR:NROW, cols(fc)], rem[2 * BCR:NROW, 1, :]).then_inc(S["low_ok"], 1)

                def inputs(b, k):
                    ch, sl = k // NS, k % 2
                    wait(dve, "b_mm", b, k + 1)
                    if k % NS == 0:
                        wait(dve, "du_ok", b, NH * (ch + 1))
                    wait(dve, "h_ok", b, 2 * (k - 1))
                    dve.tensor_tensor(dbu[:, sl, :, :], psR[:, :].unsqueeze(1).to_broadcast([128, NH, CH]),
                                      du[:, :, cols(ch)], ALU.mult).then_inc(S["dbu_ok"], 1)

                def scans(b, k):
                    ch, n_ = divmod(k, NS)
                    sl = k % 2
                    wait(dve, "prod", b, k - 1)
                    wait(dve, "hlast_ok", b, min(k - 1, NS))
                    if ch:
                        wait(dve, "hlast_ok", b, n_ + 1)
                    wait(dve, "dbu_ok", b, k + 1)
                    for h in range(NH):
                        wait(dve, "da_ok", b, 2 * k + h + 1)
                        dve.tensor_tensor_scan(hs[:, sl, h, :], da[:, sl, h, :], dbu[:, sl, h, :],
                                               hlast[:, n_, h:h + 1] if ch else 0.0, ALU.mult, ALU.add
                                               ).then_inc(S["h_ok"], 1)

                def gate(b, ch):
                    wait(dve, "pair_mm", b, NS // 2 * (ch + 1))
                    dve.tensor_tensor(g[:, :, cols(ch)], psY[:, :, :], sz[:, :, cols(ch)], ALU.mult
                                      ).then_inc(S["g_ok"], 1)

                def normalise(a, o):
                    if o - 1 in TILE_STEP:
                        m, t = TILE_STEP[o - 1]
                        i = TILES * m + t
                        sl = i % 2
                        wait(dve, "p_ok", a, i + 1)
                        dve.reciprocal(rinv[:, sl:sl + 1], rsum[:, sl:sl + 1]).then_inc(S["rinv_ok"], 1)
                        wait(dve, "rinv_ok", a, i + 1)
                        dve.tensor_scalar(p[:, sl, :], p[:, sl, :], rinv[:, sl:sl + 1], None, ALU.mult
                                          ).then_inc(S["pn_ok"], 1)

                def query(a, m):
                    wait(dve, "q_mm", a, m + 1)
                    if m == 0:
                        dve.tensor_scalar(qa[:, :], flat(psE), c_bq, None, ALU.add).then_inc(S["q_ok"], 1)
                    else:
                        dve.tensor_scalar(qa[0:HD, :], flat(psE)[0:HD, :], float(C) ** -0.5, None, ALU.mult
                                          ).then_inc(S["q_ok"], 1)

                def row_max(a, o):
                    if o in TILE_STEP:
                        m, t = TILE_STEP[o]
                        i = TILES * m + t
                        wait(dve, "e_mm", a, i + 1)
                        wait(dve, "p_ok", a, i - 1)
                        dve.tensor_reduce(nm[:, i % 2:i % 2 + 1], flat(psE), AX, ALU.max, negate=True
                                          ).then_inc(S["nm_ok"], 1)

                def attended(a, o):
                    if o - 3 in TILE_STEP and TILE_STEP[o - 3][1] % GT == GT - 1:
                        m, t = TILE_STEP[o - 3]
                        gq = t // GT
                        i = NG // 2 * m + gq
                        part = slice(gq * GL, (gq + 1) * GL)
                        wait(dve, "av_mm", a, i + 1)
                        if m == 0:
                            if gq == 0:
                                at(dve, "x2_out", a * 16)
                            wait(dve, "x1g_ok", a, NCH)
                            dve.scalar_tensor_tensor(out=x2[:, part], in0=psA[:, 0:GL], scalar=c_gam, in1=x1g[:, part],
                                                     op0=ALU.mult, op1=ALU.add).then_inc(S["out_ok"], 1)
                        else:
                            if gq == 0:
                                at(dve, "f_out", a * 16)
                            dve.tensor_copy(fa[:, part], psA[:, 0:GL]).then_inc(S["out_ok"], 1)
                            wait(dve, "out_ok", a, i + 1)
                            dve.bn_stats(bst[:, bass.ds(a, 1), gq, :].rearrange("p a s -> p (a s)"), fa[:, part]
                                         ).then_inc(S["bn_ok"], 1)

                def image(b, scan, more, att, late):
                    for c in range(NCH):
                        for r in range(NS):
                            k = NS * c + r
                            now = [(b - 1, k)] if att else []
                            if late and k < LATE:
                                now.append((b - 2, 2 * NS + k))
                            if scan:
                                inputs(b, k)
                            for a, o in now:
                                normalise(a, o)
                            if att and k == 2:
                                gate(b - 1, 1)
                            if scan and k == NS + 2:
                                gate(b, 0)
                            front_of = (b, 1) if c == 0 and scan else (b + 1, 0) if c == 1 and more else None
                            if front_of and r == AT_Z:
                                front(*front_of, r)
                            if scan:
                                scans(b, k)
                            if att and r == AT_Q + 1:
                                query(b - 1, c)
                            for a, o in now:
                                if r == AT_Z + 1:
                                    attended(a, o)
                            if front_of and r != AT_Z:
                                front(*front_of, r)
                            for a, o in now:
                                row_max(a, o)
                                if r != AT_Z + 1:
                                    attended(a, o)

                for r in range(NS):
                    front(0, 0, r)
                image(0, True, True, False, False)
                image(1, True, True, True, False)
                with dve.Fori(2, NB - 1) as b:
                    image(b, True, True, True, True)
                image(NB - 1, True, False, True, True)
                image(NB, False, False, True, True)
                image(NB + 1, False, False, False, True)

                wait(dve, "bn_ok", NB, 0)
                n[0] = 0
                link(dve.bn_aggr(mv[:, :], bst[:, :, :, :].rearrange("p b q s -> p (b q s)")), "fin_chain")
                link(dve.tensor_scalar(c_v2, mv[:, 1:2], EPS_BN, None, ALU.add), "fin_chain")
                dve.wait_ge(S["fin_act"], 1)
                link(dve.reciprocal(c_rs, c_rs), "fin_chain")
                link(dve.tensor_tensor(c_s, c_rs, c_bng, ALU.mult), "fin_chain")
                link(dve.tensor_tensor(c_t, mv[:, 0:1], c_s, ALU.mult), "fin_chain")
                link(dve.tensor_tensor(c_t, c_bnb, c_t, ALU.subtract), "fin_chain")

                def fin(i):
                    for k in range(SLOTS):
                        at(dve, "fscaled", i * SLOTS + k + 1)
                        dve.tensor_tensor(fbuf[k], fbuf[k], xbuf[k], ALU.add).then_inc(S["fsum"], 1)

                fin(0)
                with dve.Fori(1, ROUNDS) as i:
                    fin(i)

            @block.scalar
            def _(act):
                act.wait_ge(S["weights_in"], 16 * len(PARAMS))
                act.wait_ge(S["xl0"], 16)
                act.activation(x1[:, :], xin[:, :], ACT.Copy, accum_out=c_mean).then_inc(S["mean0"], 1)
                act.activation(neg_a[:, :, :], neg_a[:, :, :], ACT.Exp).then_inc(S["mean0"], 1)
                act.wait_ge(S["mean0"], 3)

                def centre(i, k):
                    n = i * 2 + k
                    at(act, f"xl{k}", (i + 1) * 16)
                    at(act, "st_turned", 2 * (n - 1))
                    act.activation(centred[k][:, :], slots[k][:, :], ACT.Identity, bias=c_nshift,
                                   accum_out=sums[:, bass.ds(n, 1)]).then_inc(S["st_centred"], 1)

                centre(0, 0)
                centre(0, 1)
                with act.Fori(1, NB // 2) as i:
                    centre(i, 0)
                    centre(i, 1)

                for j in range(4):
                    act.wait_ge(S["stats_chain"], mark["pivot", j])
                    act.sqrt(q0[:, 90:91], q0[:, 89:90]).then_inc(S["stats_act"], 1)
                act.wait_ge(S["stats_chain"], mark["m0_done"])

                def front(fb, fc, r):
                    if r == AT_C:
                        wait(act, "cent_mm", fb, fc + 1)
                        wait(act, "xn_ok", fb, fc)
                        act.activation(xcen[:, :], psT[:, 0, :], ACT.Identity, bias=c_cc).then_inc(S["xcen_ok"], 1)
                        act.activation(sq[:, :], psT[:, 0, :], ACT.Square, bias=c_cc).then_inc(S["sq_ok"], 1)
                    if r == AT_C + 1:
                        wait(act, "var_mm", fb, fc + 1)
                        act.activation(lnv[:, :], psE[:, 0, :], ACT.Ln, bias=c_v).then_inc(S["lnv_ok"], 1)
                        wait(act, "lnv_ok", fb, fc + 1)
                        act.activation(rstd[:, :], lnv[:, :], ACT.Exp, scale=-0.5).then_inc(S["rs_ok"], 1)
                    if r == AT_X:
                        for h in range(NH):
                            wait(act, "xi_mm", fb, 2 * fc + h + 1)
                            lo = KC - 1 + fc * CH
                            act.activation(xi[:, h, lo:lo + CH], psT[:, h, :], ACT.Identity, bias=c_wb[:, h:h + 1]
                                           ).then_inc(S["xi_ok"], 1)
                    if r == AT_Z:
                        for h in range(NH):
                            wait(act, "conv", fb, 4 * (2 * fc + h) + 4)
                            act.activation(xc[:, h, cols(fc)], xc[:, h, cols(fc)], ACT.Silu).then_inc(S["xc_ok"], 1)
                        for h in range(NH):
                            wait(act, "z_mm", fb, 2 * fc + h + 1)
                            act.activation(sz[:, h, cols(fc)], psT[:, h, :], ACT.Silu, bias=c_wb[:, NH + h:NH + h + 1]
                                           ).then_inc(S["z_ok"], 1)
                        act.preload_act_table_set("natural_log_exp_and_others")
                    if r == AT_Z + 1:
                        wait(act, "dbl_mm", fb, fc + 1)
                        act.activation(bc[0:NROW, cols(fc)], psE[0:NROW, 0, :], ACT.Copy).then_inc(S["hi_ok"], 1)
                    if r == AT_P:
                        wait(act, "r1_ok", fb, fc + 1)
                        act.activation(bc[BCR:2 * BCR, cols(fc)], rem[BCR:2 * BCR, 0, :], ACT.Copy).then_inc(S["midb_ok"], 1)
                        for h in range(NH):
                            wait(act, "dpre_mm", fb, 2 * fc + h + 1)
                            act.activation(sp_e[:, h, :], psT[:, h, :], ACT.Abs, bias=c_bdt[:, h:h + 1]
                                           ).then_inc(S["sp_abs"], 1)
                            act.activation(delta[:, h, cols(fc)], psT[:, h, :], ACT.Relu, bias=c_bdt[:, h:h + 1]
                                           ).then_inc(S["sp_relu"], 1)
                    if r in (AT_P + 1, AT_P + 2):
                        h = r - AT_P - 1
                        wait(act, "sp_abs", fb, 2 * fc + h + 1)
                        act.activation(sp_e[:, h, :], sp_e[:, h, :], ACT.Exp, scale=-1.0).then_inc(S["sp_exp"], 1)
                        wait(act, "sp_exp", fb, 2 * fc + h + 1)
                        act.activation(sp_l[:, h, :], sp_e[:, h, :], ACT.Ln, bias=1.0).then_inc(S["sp_ln"], 1)

                def decay(b, k):
                    ch, n = divmod(k, NS)
                    for h in range(NH):
                        if n == 0:
                            wait(act, "delta_ok", b, NH * ch + h + 1)
                        wait(act, "h_ok", b, 2 * (k - 2) + h + 1)
                        act.activation(da[:, k % 2, h, :], delta[:, h, cols(ch)], ACT.Exp,
                                       scale=neg_a[:, h, n:n + 1]).then_inc(S["da_ok"], 1)

                def c_row(b, k):
                    wait(act, "c_mm", b, k + 1)
                    wait(act, "prod", b, k - 1)
                    act.activation(cs[:, k % 2, :], psR[:, :], ACT.Copy).then_inc(S["c_ok"], 1)

                def turned_out(a, o):
                    if o - 1 in TILE_STEP:
                        m, t = TILE_STEP[o - 1]
                        i = TILES * m + t
                        for q in range(2):
                            wait(act, "turn", a, 2 * i + q + 1)
                            if t % GT == 0:
                                wait(act, "av_mm", a, i // GT - 1)
                            act.activation(pt[:, i // GT % 2, 4 * q:4 * q + 4, 128 * (t % GT):128 * (t % GT) + 128],
                                           psT[:, q, :].rearrange("p (j i) -> p j i", j=4), ACT.Copy
                                           ).then_inc(S["pt_ok"], 1)

                def key(a, m):
                    wait(act, "k_mm", a, m + 1)
                    if m == 0:
                        act.activation(ka[:, :], flat(psT), ACT.Identity, bias=c_bk).then_inc(S["k_ok"], 1)
                    else:
                        act.activation(ka[0:HD, :], flat(psT)[0:HD, :], ACT.Copy).then_inc(S["k_ok"], 1)

                def value(a, m):
                    wait(act, "v_mm", a, m + 1)
                    act.activation(va[:, :, :], split(psT), ACT.Copy).then_inc(S["v_ok"], 1)

                def residual(b, ch):
                    wait(act, "x1_mm", b, ch + 1)
                    act.activation(x1[:, cols(ch)], psE[:, 1, :], ACT.Identity, bias=c_c0).then_inc(S["x1_ok"], 1)
                    wait(act, "out_ok", b - 1, NG // 4 * (ch + 1))
                    act.activation(x1g[:, cols(ch)], psE[:, 1, :], ACT.Identity, bias=c_c0g).then_inc(S["x1g_ok"], 1)

                def numer(a, o):
                    if o in TILE_STEP:
                        m, t = TILE_STEP[o]
                        i = TILES * m + t
                        wait(act, "nm_ok", a, i + 1)
                        wait(act, "turn", a, 2 * (i - 1))
                        act.activation(p[:, i % 2, :], flat(psE), ACT.Exp, bias=nm[:, i % 2:i % 2 + 1],
                                       accum_out=rsum[:, i % 2:i % 2 + 1]).then_inc(S["p_ok"], 1)

                def image(b, scan, more, att, late):
                    for c in range(NCH):
                        for r in range(NS):
                            k = NS * c + r
                            now = [(b - 1, k)] if att else []
                            if late and k < LATE:
                                now.append((b - 2, 2 * NS + k))
                            front_of = (b, 1) if c == 0 and scan else (b + 1, 0) if c == 1 and more else None
                            if scan:
                                c_row(b, k)
                            if att and r == AT_Q + 1:
                                key(b - 1, c)
                            if att and r == AT_V + 1:
                                value(b - 1, c)
                            score_now = any(o in TILE_STEP for a, o in now)
                            for a, o in now:
                                if not score_now:
                                    turned_out(a, o)
                            if front_of and r == AT_Z + 1:
                                front(*front_of, r)
                            if scan and (k < STEPS - 1 or more):
                                decay(*((b, k + 1) if k < STEPS - 1 else (b + 1, 0)))
                            if att and k == AT_R:
                                residual(b - 1, 1)
                            if scan and k == NS + AT_R:
                                residual(b, 0)
                            if front_of and r < AT_P and r != AT_Z + 1:
                                front(*front_of, r)
                            for a, o in now:
                                if score_now:
                                    turned_out(a, o)
                            for a, o in now:
                                numer(a, o)
                            if front_of and r >= AT_P:
                                front(*front_of, r)

                for r in range(NS):
                    front(0, 0, r)
                decay(0, 0)
                image(0, True, True, False, False)
                image(1, True, True, True, False)
                with act.Fori(2, NB - 1) as b:
                    image(b, True, True, True, True)
                image(NB - 1, True, False, True, True)
                image(NB, False, False, True, True)
                image(NB + 1, False, False, False, True)

                act.wait_ge(S["fin_chain"], 2)
                act.sqrt(c_rs, c_v2).then_inc(S["fin_act"], 1)
                act.wait_ge(S["fin_chain"], 6)

                def images(dram, i, k):
                    return dram[bass.ds(2 * (i * SLOTS + k), 2), :, :].rearrange("a c l -> c a l")

                def fin(i):
                    for k in range(SLOTS):
                        at(act, f"fl{k}", 32 * (i + 1))
                        act.activation(fbuf[k], fbuf[k], ACT.Identity, bias=c_t, scale=c_s).then_inc(S["fscaled"], 1)
                        if k:
                            store(i, k - 1)
                    store(i, SLOTS - 1)

                def store(i, k):
                    at(act, "fsum", i * SLOTS + k + 1)
                    act.dma_start(images(out, i, k), fbuf[k]).then_inc(S[f"out{k}"], 16)

                fin(0)
                with act.Fori(1, ROUNDS) as i:
                    fin(i)

            @block.tensor
            def _(pe):
                def mm(dst, lhsT, rhs, start=True, stop=True):
                    return pe.matmul(dst, lhsT, rhs, start=start, stop=stop)

                def wide(dst, lhsT, rhs, rows=128):
                    for c in range(NCH):
                        last = mm(dst[0:rows, c, :], lhsT, rhs[:, c * CH:(c + 1) * CH])
                    return last

                pe.wait_ge(S["weights_in"], 16 * len(PARAMS))
                pe.wait_ge(S["consts_made"], mark["consts"])
                for e in range(4):
                    last = mm(psY[:, 0, e:e + 1], w_in_t[:, 128 * e:128 * e + 128], c_lnb)
                last.then_inc(S["pe_setup"], 1)

                def stat(i, k):
                    m = i * 2 + k
                    at(pe, "st_centred", m + 1)
                    for q in range(2):
                        at(pe, "st_copied", 2 * (m - 1) + q + 1)
                        for j in range(4):
                            last = pe.transpose(psT[:, q, 128 * j:128 * j + 128],
                                                centred[k][:, (4 * q + j) * 128:(4 * q + j + 1) * 128], ident[:, :])
                        last.then_inc(S["st_turned"], 1)
                    at(pe, "st_added", m - 1)
                    for q in range(2):
                        at(pe, "st_copied", 2 * m + q + 1)
                        for j in range(4):
                            blk = turned[q][:, 128 * j:128 * j + 128]
                            last = mm((psR[:, 0:128], psY[:, 1, 0:128])[k], blk, blk, start=(q == 0 and j == 0), stop=(q == 1 and j == 3))
                    last.then_inc(S["st_gram"], 1)

                stat(0, 0)
                stat(0, 1)
                with pe.Fori(1, NB // 2) as i:
                    stat(i, 0)
                    stat(i, 1)
                pe.wait_ge(S["stats_chain"], mark["gathered"])
                for i in range(4):
                    last = mm(psT[0:32, 0, 5 * i:5 * i + 5], ident[:, 32 * i:32 * i + 32], dcov[:, :])
                last.then_inc(S["pe_setup"], 1)
                pe.wait_ge(S["stats_chain"], mark["mixed"])
                for k in range(4):
                    last = mm(psT[32 * k:32 * k + 32, 1, 0:4], ident[0:32, 0:32], q0[:, 52 + 4 * k:56 + 4 * k])
                last.then_inc(S["pe_setup"], 1)
                pe.wait_ge(S["stats_chain"], mark["m0"])
                pe.transpose(psY[:, 1, 0:128], m0[:, :], ident[:, :])
                mm(psY[:, 0, 0:1], m0[:, :], c_mean).then_inc(S["pe_setup"], 1)
                pe.wait_ge(S["stats_chain"], mark["m0_rows"])
                mm(psT[:, 0, 0:128], m0_rows[:, :], cent[:, :])
                mm(psT[:, 1, 0:1], cent[:, :], c_c0).then_inc(S["pe_setup"], 1)
                pe.wait_ge(S["stats_chain"], mark["m0_done"])

                def front(what, fb, fc, att):
                    if what == "centre":
                        at(pe, "x_in", 16 * (fb + 1))
                        wait(pe, "sp_relu", fb, 2 * fc)
                        if att:
                            wait(pe, "pt_ok", *att["turned7"])
                        mm(psT[:, 0, :], m0c[:, :], xin[:, cols(fc)]).then_inc(S["cent_mm"], 1)
                    if what == "gates":
                        if att:
                            wait(pe, "pt_ok", *att["turned1"])
                        else:
                            wait(pe, "xi_ok", fb, 2 * fc + 2)
                        for h in range(NH):
                            mm(psT[:, h, :], w_in_t[:, DI + C * h:DI + C * h + C], xn[:, :]).then_inc(S["z_mm"], 1)
                    if what == "steps":
                        wait(pe, "dt_ok", fb, fc + 1)
                        wait(pe, "z_ok", fb, 2 * fc + 2)
                        for h in range(NH):
                            mm(psT[:, h, :], w_dt_t[NROW:NROW + DR, C * h:C * h + C], dts[NROW:NROW + DR, :]
                               ).then_inc(S["dpre_mm"], 1)
                    if what == "variance":
                        wait(pe, "sq_ok", fb, fc + 1)
                        if att:
                            wait(pe, "p_ok", *att["tile7"])
                        mm(psE[:, 0, :], avg[:, :], sq[:, :]).then_inc(S["var_mm"], 1)
                    if what == "inner":
                        wait(pe, "xn_ok", fb, fc + 1)
                        if att:
                            wait(pe, "k_ok", *att["k"])
                        for h in range(NH):
                            mm(psT[:, h, :], w_in_t[:, C * h:C * h + C], xn[:, :]).then_inc(S["xi_mm"], 1)
                    if what == "rows":
                        wait(pe, "xc_ok", fb, 2 * fc + 2)
                        if att:
                            wait(pe, "p_ok", *att["tile1"])
                        for h in range(NH):
                            last = mm(psE[0:NROW + DR, 0, :], w_x_t[:, h, :], xc[:, h, cols(fc)],
                                      start=(h == 0), stop=(h == NH - 1))
                        last.then_inc(S["dbl_mm"], 1)

                def b_row(b, k):
                    ch, n_ = divmod(k, NS)
                    if n_ == 0:
                        wait(pe, "low_ok", b, ch + 1)
                        wait(pe, "midb_ok", b, ch + 1)
                    wait(pe, "c_ok", b, k)
                    mm(psR[:, :], sel[0:NROW, n_, :], bc[0:NROW, cols(ch)]).then_inc(S["b_mm"], 1)

                def c_row(b, k):
                    ch, n_ = divmod(k, NS)
                    wait(pe, "dbu_ok", b, k + 1)
                    mm(psR[:, :], sel[0:NROW, NS + n_, :], bc[0:NROW, cols(ch)]).then_inc(S["c_mm"], 1)

                def sum_states(b, k):
                    pr, h = k // 2 - 1, k % 2
                    ch, q = divmod(pr, NS // 2)
                    if q == 0 and h == 0:
                        wait(pe, "g_ok", b, ch)
                    wait(pe, "pair", b, pr + 1)
                    last = mm(psY[:, h, :], ident[:, :], pa[:, pr % 2, h, :], start=(q == 0), stop=(q == NS // 2 - 1))
                    if h == 1:
                        last.then_inc(S["pair_mm"], 1)

                def skip_term(b, ch):
                    wait(pe, "xc_ok", b, NH * (ch + 1))
                    for h in range(NH):
                        mm(psY[:, h, :], dp_diag[:, h, :], xc[:, h, cols(ch)], start=False, stop=False)

                def residual(b, ch, front, late):
                    wait(pe, "g_ok", b, ch + 1)
                    at(pe, f"xr_in{ch}", 16 * (b + 1))
                    if late:
                        wait(pe, "p_ok", *late)
                    mm(psE[:, 1, :], m0[:, :], xres[:, cols(ch)], stop=False)
                    for h in range(NH):
                        last = mm(psE[:, 1, :], w_out_t[:, h, :], g[:, h, cols(ch)], start=False, stop=(h == NH - 1))
                    last.then_inc(S["x1_mm"], 1)

                def energy(a, m, t, front):
                    i = TILES * m + t
                    w = C if m == 0 else HD
                    if t == 0:
                        wait(pe, "q_ok", a, m + 1)
                        wait(pe, "k_ok", a, m + 1)
                    if t == 2 and front:
                        for name in ("hi_ok", "dt_ok", "r1_ok"):
                            wait(pe, name, front[0], front[1] + 1)
                    wait(pe, "p_ok", a, i)
                    for c in range(NCH):
                        last = mm(psE[:, c, :], qa[0:w, 128 * t:128 * t + 128], ka[0:w, cols(c)])
                    last.then_inc(S["e_mm"], 1)

                def turn(a, m, t, front):
                    i = TILES * m + t
                    wait(pe, "pn_ok", a, i + 1)
                    if t == 0:
                        wait(pe, "v_ok", a, m + 1)
                    if t == 2 and front:
                        wait(pe, "sp_relu", front[0], 2 * front[1] + 2)
                    for q in range(2):
                        wait(pe, "pt_ok", a, 2 * (i - 1) + q + 1)
                        for j in range(4):
                            last = pe.transpose(psT[:, q, 128 * j:128 * j + 128],
                                                p[:, i % 2, (4 * q + j) * 128:(4 * q + j + 1) * 128], ident[:, :])
                        last.then_inc(S["turn"], 1)

                def values(a, m, t, half):
                    i = (TILES * m + t) // GT
                    if half == 0:
                        wait(pe, "out_ok", a, i)
                    wait(pe, "pt_ok", a, 2 * GT * (i + 1) - 1 + half)
                    for j in range(TB // 2 * half, TB // 2 * (half + 1)):
                        last = mm(psA[:, 0:GL], va[:, j, :], pt[:, i % 2, j, :], start=(j == 0), stop=(j == TB - 1))
                    if half:
                        last.then_inc(S["av_mm"], 1)

                def project(a, m, c, front, other):
                    w = C if m == 0 else HD
                    (src, wq, wk) = ((x1, w_q_t, w_k_t), (x2, th_t, ph_t))[m]
                    if m == 0:
                        wait(pe, "x1_ok", a, c + 1)
                    else:
                        wait(pe, "out_ok", a, (c + 1) * NG // 4)
                    if c == 0:
                        if front:
                            wait(pe, "lnv_ok", front[0], front[1] + 1)
                        if m == 0 and other:
                            wait(pe, "pt_ok", a - 1, 4 * TILES)
                        if m == 1:
                            wait(pe, "p_ok", a, TILES)
                    elif m == 0:
                        wait(pe, "x1g_ok", a, NCH)
                    elif other:
                        wait(pe, "x1g_ok", a + 1, 1)
                    last = mm(psT[0:w, c, :], wk[:, :], src[:, cols(c)])
                    if c == NCH - 1:
                        last.then_inc(S["k_mm"], 1)
                    last = mm(psE[0:w, c, :], wq[:, :], src[:, cols(c)])
                    if c == NCH - 1:
                        last.then_inc(S["q_mm"], 1)

                def project_values(a, m, front):
                    if front:
                        wait(pe, "xi_ok", front[0], 2 * front[1] + 2)
                    wait(pe, "k_ok", a, m + 1)
                    src, w = ((x1, w_v_t), (x2, cv_t))[m]
                    for j in range(TB):
                        last = mm(split(psT)[:, j, :], src[:, 128 * j:128 * j + 128], w[:, :])
                    last.then_inc(S["v_mm"], 1)

                ORDER = [
                    ("weigh", "energy", "turn add"),
                    ("weigh", "turn", "add"),
                    ("centre", "weigh", "add"),
                    ("weigh", "residual", "add variance"),
                    ("", "project0", "add project1"),
                    ("", "add", "inner"),
                    ("", "energy", "project_values add"),
                    ("", "energy", "turn add"),
                    ("", "turn", "skip add"),
                    ("gates", "add", "weigh"),
                    ("weigh", "rows", "add"),
                    ("steps", "energy", "add"),
                    ("", "energy", "turn add"),
                    ("", "energy", "turn add"),
                    ("weigh", "energy", "turn add"),
                    ("weigh", "energy", "turn add"),
                ]
                FRONT = ("centre", "variance", "inner", "gates", "rows", "steps")

                def image(b, scan, more, att, late):
                    for c in range(NCH):
                        if c == 0:
                            front_of = (b, 1) if scan else None
                            old = (b - 2, 1) if late else None
                        else:
                            front_of = (b + 1, 0) if more else None
                            old = (b - 1, 0) if att else None
                        beside = {}
                        if old:
                            beside.update(turned7=(old[0], 16 * old[1] + 16), tile7=(old[0], 8 * old[1] + 8))
                        if att:
                            beside.update(k=(b - 1, c + 1), turned1=(b - 1, 16 * c + 4), tile1=(b - 1, 8 * c + 2))
                        for r in range(NS):
                            k = NS * c + r
                            now = [(b - 1, k)] if att else []
                            if late and k < LATE:
                                now.append((b - 2, 2 * NS + k))
                            need = beside if (old if r in (AT_C, AT_R) else att) else None

                            def work(names):
                                for what in names.split():
                                    if what in FRONT:
                                        if front_of:
                                            front(what, *front_of, need)
                                    elif what == "add":
                                        if scan and k >= 2:
                                            sum_states(b, k)
                                        elif att and k < 2:
                                            sum_states(b - 1, STEPS + k)
                                    elif what == "skip":
                                        if scan:
                                            skip_term(b, c)
                                    elif what == "residual":
                                        if att and c == 0:
                                            residual(b - 1, 1, front_of, (b - 2, 16) if late else None)
                                        if scan and c == 1:
                                            residual(b, 0, front_of, (b - 1, 8) if att else None)
                                    elif what in ("project0", "project1"):
                                        if att:
                                            project(b - 1, c, int(what == "project1"), front_of, late if c == 0 else scan)
                                    elif what == "project_values":
                                        if att:
                                            project_values(b - 1, c, front_of)
                                    for a, o in now:
                                        if what == "energy" and o in TILE_STEP:
                                            energy(a, *TILE_STEP[o], front_of)
                                        if what == "turn" and o - 1 in TILE_STEP:
                                            turn(a, *TILE_STEP[o - 1], front_of)
                                        for half in range(2):
                                            last_tile = o - 2 - half
                                            if what == "weigh" and last_tile in TILE_STEP and TILE_STEP[last_tile][1] % GT == GT - 1:
                                                values(a, *TILE_STEP[last_tile], half)

                            before, between, after = ORDER[r]
                            work(before)
                            if scan:
                                c_row(b, k)
                            work(between)
                            if scan and (k < STEPS - 1 or more):
                                b_row(*((b, k + 1) if k < STEPS - 1 else (b + 1, 0)))
                            work(after)

                for what in FRONT:
                    front(what, 0, 0, None)
                b_row(0, 0)
                image(0, True, True, False, False)
                image(1, True, True, True, False)
                with pe.Fori(2, NB - 1) as b:
                    image(b, True, True, True, True)
                image(NB - 1, True, False, True, True)
                image(NB, False, False, True, True)
                image(NB + 1, False, False, False, True)

            @block.sync
            def _(sp):
                for dst, src in PARAMS:
                    sp.dma_start(dst, src).then_inc(S["weights_in"], 16)

                def load_stat(i, k):
                    at(sp, "st_centred", i * 2 + k - 1)
                    sp.dma_start(slots[k][:, :], x[bass.ds(i * 2 + k, 1), :, :].rearrange("a c l -> c (a l)")
                                 ).then_inc(S[f"xl{k}"], 16)

                load_stat(0, 0)
                load_stat(0, 1)
                with sp.Fori(1, NB // 2) as i:
                    load_stat(i, 0)
                    load_stat(i, 1)
                at(sp, "st_centred", NB)

                def load_x(b):
                    sp.dma_start(xin[:, :], x[bass.ds(b, 1), :, :].rearrange("a c l -> c (a l)")).then_inc(S["x_in"], 16)

                def load_residual(b, c):
                    sp.dma_start(xres[:, cols(c)], x[bass.ds(b, 1), :, cols(c)].rearrange("a c l -> c (a l)")
                                 ).then_inc(S[f"xr_in{c}"], 16)

                def image(b, scan, more, att, late):
                    if late:
                        wait(sp, "bn_ok", b - 2, NG // 2)
                        sp.dma_start(f_dram[bass.ds(b - 2, 1), :, :].rearrange("a c l -> c (a l)"), fa[:, :]
                                     ).then_inc(S["f_out"], 16)
                    if att and scan:
                        wait(sp, "x1_mm", b - 1, 2)
                        load_residual(b, 1)
                    if more:
                        wait(sp, "cent_mm", b, 2)
                        load_x(b + 1)
                    if scan:
                        wait(sp, "x1_mm", b, 1)
                        if more:
                            load_residual(b + 1, 0)
                    if att:
                        wait(sp, "out_ok", b - 1, NG // 2)
                        sp.dma_start(x2_dram[bass.ds(b - 1, 1), :, :].rearrange("a c l -> c (a l)"), x2[:, :]
                                     ).then_inc(S["x2_out"], 16)

                load_x(0)
                load_residual(0, 0)
                load_residual(0, 1)
                image(0, True, True, False, False)
                image(1, True, True, True, False)
                with sp.Fori(2, NB - 1) as b:
                    image(b, True, True, True, True)
                image(NB - 1, True, False, True, True)
                image(NB, False, False, True, True)
                image(NB + 1, False, False, False, True)

                at(sp, "f_out", 16 * NB)
                at(sp, "x2_out", 16 * NB)
                at(sp, "fin_chain", 6)

                def images(dram, i, k):
                    return dram[bass.ds(2 * (i * SLOTS + k), 2), :, :].rearrange("a c l -> c a l")

                def load_fin(i):
                    for k in range(SLOTS):
                        at(sp, f"out{k}", 16 * i)
                        sp.dma_start(fbuf[k], images(f_dram, i, k)).then_inc(S[f"fl{k}"], 16)
                        sp.dma_start(xbuf[k], images(x2_dram, i, k)).then_inc(S[f"fl{k}"], 16)

                load_fin(0)
                with sp.Fori(1, ROUNDS) as i:
                    load_fin(i)
                for k in range(SLOTS):
                    at(sp, f"out{k}", 16 * ROUNDS)


def kernel(x, L0_conv_weight, L0_conv_bias, L1_conv_ln_w, L1_conv_ln_b, L1_conv_W_in, L1_conv_conv_w, L1_conv_conv_b,
           L1_conv_W_x, L1_conv_W_dt, L1_conv_b_dt, L1_conv_A_log, L1_conv_Dp, L1_conv_W_out, L2_conv_Wq, L2_conv_bq,
           L2_conv_Wk, L2_conv_bk, L2_conv_Wv, L2_conv_bv, L2_conv_gamma, L3_conv_theta_w, L3_conv_phi_w, L3_conv_conv_w,
           L3_conv_gamma, L3_conv_beta):
    import numpy as np
    import concourse.bacc as bacc
    from concourse.bass_utils import run_bass_kernel_spmd

    def col(v):
        return np.asarray(v).reshape(C, 1)

    def halves(v):
        v = np.asarray(v).reshape(NH, C, -1).transpose(1, 0, 2)
        return v

    arrays = dict(
        x=np.asarray(x).reshape(NB, C, L),
        w0=np.asarray(L0_conv_weight).transpose(2, 0, 1), b0=col(L0_conv_bias), ln_w=col(L1_conv_ln_w), ln_b=col(L1_conv_ln_b),
        w_in=np.asarray(L1_conv_W_in).T, conv_w=halves(L1_conv_conv_w), conv_b=halves(L1_conv_conv_b)[:, :, 0],
        w_x=halves(np.asarray(L1_conv_W_x).T), w_dt=np.asarray(L1_conv_W_dt).T, b_dt=halves(L1_conv_b_dt)[:, :, 0],
        a_log=halves(L1_conv_A_log), dp=halves(L1_conv_Dp)[:, :, 0], w_out=halves(np.asarray(L1_conv_W_out).T),
        w_q=np.asarray(L2_conv_Wq).T, b_q=col(L2_conv_bq), w_k=np.asarray(L2_conv_Wk).T, b_k=col(L2_conv_bk),
        w_v=np.asarray(L2_conv_Wv).T, b_v=col(L2_conv_bv), gam=np.asarray(L2_conv_gamma).reshape(1, 1),
        th_w=np.asarray(L3_conv_theta_w).T, ph_w=np.asarray(L3_conv_phi_w).T, cv_w=np.asarray(L3_conv_conv_w).T,
        bn_g=col(L3_conv_gamma), bn_b=col(L3_conv_beta),
    )
    arrays = {k: np.ascontiguousarray(v) for k, v in arrays.items()}
    nc = bacc.Bacc("TRN2", target_bir_lowering=False, num_devices=1)
    aps = {k: nc.dram_tensor(k, v.shape, mybir.dt.from_np(v.dtype), kind="ExternalInput").ap() for k, v in arrays.items()}
    out = nc.dram_tensor("out", (NB, C, L), mybir.dt.float32, kind="ExternalOutput").ap()
    build(nc, out=out, **aps)
    result = run_bass_kernel_spmd(nc, [arrays], core_ids=[0])
    return result.results[0]["out"].reshape(NB, C, HH, WW)
```

```python
from contextlib import ExitStack

import concourse.bass as bass
from concourse import mybir

NB, C, HH, WW = 32, 128, 32, 32
L = HH * WW
F = C // 4
DI = 2 * C
NH = DI // C
NS = 16
KC = 4
DR = C // 16
CH = 512
NCH = L // CH
BCR = 2 * NS
NROW = 3 * BCR
TB = L // 128
HD = C // 2
STEPS = NCH * NS
TILES = TB
GT = 2
NG = 2 * TILES // GT
GL = GT * 128
EPS0, EPS_LN, EPS_BN = 1e-5, 1e-5, 1e-5


def build(nc, x, w0, b0, ln_w, ln_b, w_in, conv_w, conv_b, w_x, w_dt, b_dt, a_log, dp, w_out,
          w_q, b_q, w_k, b_k, w_v, b_v, gam, th_w, ph_w, cv_w, bn_g, bn_b, out):
    fp32, bf16 = mybir.dt.float32, mybir.dt.bfloat16
    ALU = mybir.AluOpType
    ACT = mybir.ActivationFunctionType
    AX = mybir.AxisListType.X
    ctx = ExitStack()
    with ctx:
        def sb(name, shape, dt=fp32):
            return ctx.enter_context(nc.sbuf_tensor(name, shape, dt))

        def pb(name, shape):
            return ctx.enter_context(nc.psum_tensor(name, shape, fp32))

        def sem(name):
            return ctx.enter_context(nc.semaphore(name))

        x2_dram = nc.dram_tensor("x2_scratch", [NB, C, L], fp32).ap()
        f_dram = nc.dram_tensor("f_scratch", [NB, C, L], fp32).ap()

        ident = sb("ident", [128, 128])
        mask32 = sb("mask32", [128, 32])
        sel = sb("sel", [128, BCR, 128], bf16)
        cent = sb("cent", [128, 128])
        avg = sb("avg", [128, 128])
        m0 = sb("m0", [128, 128])
        m0_rows = sb("m0_rows", [128, 128])
        m0c = sb("m0c", [128, 128])
        w_in_t = sb("w_in_t", [128, 2 * DI])
        w_x_t = sb("w_x_t", [128, NH, NROW + DR])
        w_dt_t = sb("w_dt_t", [128, DI])
        w_out_t = sb("w_out_t", [128, NH, C])
        w_q_t = sb("w_q_t", [128, C])
        w_k_t = sb("w_k_t", [128, C])
        w_v_t = sb("w_v_t", [128, C])
        th_r = sb("th_r", [HD, C])
        ph_r = sb("ph_r", [HD, C])
        tp_t = sb("tp_t", [128, C])
        cv_t = sb("cv_t", [128, C])
        dp_diag = sb("dp_diag", [128, NH, 128])
        cvec = sb("cvec", [128, 32])
        neg_a = sb("neg_a", [128, NH, NS])
        taps = sb("taps", [128, NH, KC])
        (c_b0, c_lnw, c_lnb, c_bq, c_bk, c_bv, c_gam, c_bng, c_bnb, c_c0, c_nshift, c_mean, c_gbv,
         c_s, c_t, c_v, c_rs, c_v2, c_cc, c_c0g) = (cvec[:, i:i + 1] for i in range(20))
        c_cb, c_bdt, c_dp = (cvec[:, 20 + 2 * i:22 + 2 * i] for i in range(3))
        c_wb = cvec[:, 26:30]

        sums = sb("sums", [128, NB])
        gram = sb("gram", [128, 128])
        dcov = sb("dcov", [128, 5])
        q0 = sb("q0", [32, 96])
        w0s = sb("w0s", [32, 4, 4])
        wcol = sb("wcol", [128, 4])

        xin = sb("xin", [128, L])
        xres = sb("xres", [128, L])
        xcen = sb("xcen", [128, CH])
        sq = sb("sq", [128, CH])
        lnv = sb("lnv", [128, CH])
        rstd = sb("rstd", [128, CH])
        xn = sb("xn", [128, CH])
        xi = sb("xi", [128, NH, KC - 1 + L])
        xc = sb("xc", [128, NH, L])
        sz = sb("sz", [128, NH, L])
        sp_e = sb("sp_e", [128, NH, CH])
        sp_l = sb("sp_l", [128, NH, CH])
        rem = sb("rem", [128, 2, CH])
        dts = sb("dts", [128, CH])
        delta = sb("delta", [128, NH, L])
        du = sb("du", [128, NH, L])
        bc = sb("bc", [128, L], bf16)
        mid = sb("mid", [128, CH], bf16)
        da = sb("da", [128, 2, NH, CH])
        dbu = sb("dbu", [128, 2, NH, CH])
        hs = sb("hs", [128, 2, NH, CH])
        hlast = sb("hlast", [128, NS, NH])
        cs = sb("cs", [128, 2, CH])
        pa = sb("pa", [128, 2, NH, CH])
        pc = sb("pc", [128, NH, CH])
        x1 = sb("x1", [128, L])
        x1g = sb("x1g", [128, L])
        qa = sb("qa", [128, L])
        ka = sb("ka", [128, L])
        va = sb("va", [128, TB, C])
        p = sb("p", [128, 2, L])
        pt = sb("pt", [128, 2, TB, GL])
        fa = sb("fa", [128, L])
        x2 = sb("x2", [128, L])
        nm = sb("nm", [128, 2])
        rsum = sb("rsum", [128, 2])
        rinv = sb("rinv", [128, 2])
        bst = sb("bst", [128, NB, NG // 2, 6])
        mv = sb("mv", [128, 2])
        g = du
        fbuf = [t[:, :, :] for t in (delta, xc)] + [t[:, :, :, :].rearrange("p a h n -> p a (h n)") for t in (hs, da)]
        xbuf = [t[:, :, :] for t in (du, sz)] + [t[:, :, :, :].rearrange("p a h n -> p a (h n)") for t in (pa, dbu)]
        SLOTS = len(fbuf)
        ROUNDS = NB // (2 * SLOTS)

        psE = pb("psE", [128, 2, CH])
        psY = pb("psY", [128, NH, CH])
        psR = pb("psR", [128, CH])
        psT = pb("psT", [128, 2, CH])
        psA = pb("psA", [128, CH])

        def flat(t):
            return t[:, :, :].rearrange("p a n -> p (a n)")

        def split(t):
            return flat(t).rearrange("p (j n) -> p j n", j=TB)

        S = {}

        def s(name):
            if name not in S:
                S[name] = sem(name)
            return S[name]

        for name in ("weights_in", "consts_made", "setup_chain", "mean0", "stats_chain", "stats_act",
                     "st_centred", "st_turned", "st_copied", "st_gram",
                     "x_in", "xr_in0", "xr_in1", "x2_out", "f_out", "fin_chain", "fin_act", "pe_setup",
                     "fscaled", "fsum"):
            s(name)
        for k in range(4):
            s(f"xl{k}")
        for k in range(SLOTS):
            s(f"fl{k}")
            s(f"out{k}")

        PER = dict(
            cent_mm=NCH, xcen_ok=NCH, sq_ok=NCH, var_mm=NCH, lnv_ok=NCH, rs_ok=NCH, xn_ok=NCH,
            xi_mm=2 * NCH, xi_ok=2 * NCH, tap0=2 * NCH, conv=2 * (KC - 1) * NCH, z_mm=2 * NCH, z_ok=2 * NCH, xc_ok=2 * NCH,
            dbl_mm=NCH, dt_ok=NCH, hi_ok=NCH, r1_ok=NCH, midb_ok=NCH, mid_ok=NCH, r2_ok=NCH, low_ok=NCH,
            dpre_mm=2 * NCH, sp_abs=2 * NCH, sp_relu=2 * NCH, sp_exp=2 * NCH, sp_ln=2 * NCH,
            delta_ok=2 * NCH, du_ok=2 * NCH,
            b_mm=STEPS, c_mm=STEPS, dbu_ok=STEPS, c_ok=STEPS, da_ok=2 * STEPS, h_ok=2 * STEPS,
            hlast_ok=NS, prod=STEPS, pair=STEPS // 2, pair_mm=STEPS // 2, g_ok=NCH,
            x1_mm=NCH, x1_ok=NCH, x1g_ok=NCH,
            q_mm=1, k_mm=2, v_mm=2, q_ok=1, k_ok=2, v_ok=2,
            e_mm=16, nm_ok=16, p_ok=16, turn=32, pt_ok=32, rinv_ok=16, pn_ok=16, av_mm=NG,
            out_ok=NG, bn_ok=NG // 2,
        )
        for name in PER:
            s(name)

        def wait(eng, name, b, k):
            value = b * PER[name] + k
            if isinstance(value, int) and value <= 0:
                return
            eng.wait_ge(S[name], value)

        def at(eng, name, value):
            if isinstance(value, int) and value <= 0:
                return
            eng.wait_ge(S[name], value)

        PARAMS = [
            (w_in_t[:, :], w_in), (w_x_t[:, :, 0:BCR], w_x[:, :, DR:]), (w_x_t[:, :, BCR:2 * BCR], w_x[:, :, DR:]),
            (w_x_t[:, :, 2 * BCR:NROW], w_x[:, :, DR:]), (w_x_t[:, :, NROW:], w_x[:, :, 0:DR]),
            (w_dt_t[NROW:NROW + DR, :], w_dt), (w_out_t[:, :, :], w_out), (w_q_t[:, :], w_q), (w_k_t[:, :], w_k),
            (w_v_t[:, :], w_v), (th_r[:, :], th_w), (ph_r[:, :], ph_w), (cv_t[:, :], cv_w),
            (neg_a[:, :, :], a_log), (taps[:, :, :], conv_w), (w0s[:, :, :], w0),
            (c_b0, b0), (c_lnw, ln_w), (c_lnb, ln_b), (c_bq, b_q), (c_bk, b_k), (c_bv, b_v),
            (c_gam, gam.to_broadcast([128, 1])), (c_bng, bn_g), (c_bnb, bn_b), (c_cb, conv_b), (c_bdt, b_dt), (c_dp, dp),
        ]

        slots = [xin, xres, x1g, fa]
        centred = [x1, x2]
        turned = [qa[:, 0:CH], qa[:, CH:L]]

        TILE_AT = [6, 7, 11, 12, 13, 14, 15, 16]
        TILE_STEP = {16 * m + TILE_AT[t]: (m, t) for m in range(2) for t in range(TILES)}
        LATE = 4
        AT_C, AT_X, AT_Z, AT_P = 2, 5, 9, 11
        AT_R, AT_Q, AT_V = 3, 4, 6

        def cols(c):
            return slice(c * CH, (c + 1) * CH)

        mark = {}

        with nc.Block() as block:

            @block.gpsimd
            def _(pool):
                n = [0]

                def link(ins):
                    n[0] += 1
                    ins.then_inc(S["consts_made"], 1)
                    pool.wait_ge(S["consts_made"], n[0])

                link(pool.memset(ident[:, :], 0.0))
                link(pool.affine_select(out=ident[:, :], in_=ident[:, :], compare_op=ALU.not_equal, fill=1.0,
                                        base=0, pattern=[[-1, 128]], channel_multiplier=1))
                link(pool.memset(mask32[:, :], 0.0))
                for q in range(4):
                    link(pool.affine_select(out=mask32[:, :], in_=mask32[:, :], compare_op=ALU.not_equal, fill=1.0,
                                            base=-32 * q, pattern=[[-1, 32]], channel_multiplier=1))
                link(pool.tensor_copy(sel[:, :, :], mask32[:, :].unsqueeze(2).to_broadcast([128, BCR, 128])))
                link(pool.memset(avg[:, :], 1.0 / C))
                link(pool.tensor_tensor(cent[:, :], ident[:, :], avg[:, :], ALU.subtract))
                link(pool.memset(xi[:, :, 0:KC - 1], 0.0))
                mark["consts"] = n[0]

                def front(fb, fc, r):
                    h = {AT_P + 3: 0, AT_P + 4: 1}.get(r)
                    if h is not None:
                        i = 2 * fc + h + 1
                        wait(pool, "sp_relu", fb, i)
                        wait(pool, "sp_ln", fb, i)
                        pool.tensor_tensor(delta[:, h, cols(fc)], delta[:, h, cols(fc)], sp_l[:, h, :], ALU.add
                                           ).then_inc(S["delta_ok"], 1)
                        wait(pool, "delta_ok", fb, i)
                        wait(pool, "xc_ok", fb, i)
                        wait(pool, "x1_mm", fb - 1, fc + 1)
                        pool.tensor_tensor(du[:, h, cols(fc)], delta[:, h, cols(fc)], xc[:, h, cols(fc)], ALU.mult
                                           ).then_inc(S["du_ok"], 1)

                def products(b, k):
                    pair, sl = k // 2, k % 2
                    wait(pool, "h_ok", b, 2 * k + 2)
                    wait(pool, "c_ok", b, k + 1)
                    c_all = cs[:, sl, :].unsqueeze(1).to_broadcast([128, NH, CH])
                    if k % 2 == 0:
                        wait(pool, "pair_mm", b, pair - 1)
                        pool.tensor_tensor(pa[:, pair % 2, :, :], hs[:, sl, :, :], c_all, ALU.mult
                                           ).then_inc(S["prod"], 1)
                    else:
                        wait(pool, "pair", b, pair)
                        pool.tensor_tensor(pc[:, :, :], hs[:, sl, :, :], c_all, ALU.mult
                                           ).then_inc(S["prod"], 1)
                    if k < NS:
                        pool.tensor_copy(hlast[:, k, :], hs[:, sl, :, CH - 1]).then_inc(S["hlast_ok"], 1)
                    if k % 2 == 1:
                        wait(pool, "prod", b, k + 1)
                        pool.tensor_tensor(pa[:, pair % 2, :, :], pa[:, pair % 2, :, :], pc[:, :, :], ALU.add
                                           ).then_inc(S["pair"], 1)

                def image(b, scan, more):
                    for c in range(NCH):
                        for r in range(NS):
                            if c == 0 and scan:
                                front(b, 1, r)
                            if c == 1 and more:
                                front(b + 1, 0, r)
                            if scan:
                                products(b, NS * c + r)

                for r in range(NS):
                    front(0, 0, r)
                image(0, True, True)
                image(1, True, True)
                with pool.Fori(2, NB - 1) as b:
                    image(b, True, True)
                image(NB - 1, True, False)

            @block.vector
            def _(dve):
                dve.wait_ge(S["weights_in"], 16 * len(PARAMS))
                dve.wait_ge(S["consts_made"], mark["consts"])
                dve.wait_ge(S["mean0"], 2)
                dve.tensor_scalar(c_nshift, c_mean, -1.0 / L, None, ALU.mult).then_inc(S["mean0"], 1)
                n = [0]

                def link(ins, name="stats_chain"):
                    n[0] += 1
                    ins.then_inc(S[name], 1)
                    dve.wait_ge(S[name], n[0])

                dve.wait_ge(S["pe_setup"], 1)
                link(dve.tensor_copy(c_wb, psY[:, 0, 0:4]))
                link(dve.tensor_scalar(tp_t[:, :], psA[:, 0:C], float(C) ** -0.5, None, ALU.mult))
                link(dve.tensor_scalar(w_in_t[:, :], w_in_t[:, :], c_lnw, None, ALU.mult))
                link(dve.tensor_scalar(neg_a[:, :, :], neg_a[:, :, :], -1.0, None, ALU.mult))
                for h in range(NH):
                    link(dve.tensor_scalar(dp_diag[:, h, :], ident[:, :], c_dp[:, h:h + 1], None, ALU.mult))
                link(dve.tensor_tensor(c_gbv, c_gam, c_bv, ALU.mult))
                link(dve.memset(c_v, EPS_LN))

                def stat(m):
                    for q in range(2):
                        at(dve, "st_turned", 2 * m + q + 1)
                        at(dve, "st_gram", 2 * m + q - 1)
                        dve.tensor_copy(turned[q], psT[:, q, :]).then_inc(S["st_copied"], 1)

                stat(0)
                with dve.Fori(1, NB) as m:
                    stat(m)
                dve.wait_ge(S["st_gram"], 2 * NB)
                dve.wait_ge(S["st_centred"], NB)
                link(dve.tensor_copy(gram[:, :], psR[:, 0:128]))

                for j in range(4):
                    link(dve.tensor_tensor(gram[:, 32 * j:32 * j + 32], gram[:, 32 * j:32 * j + 32], mask32[:, :], ALU.mult))
                    link(dve.reduce_sum(dcov[:, j:j + 1], gram[:, 32 * j:32 * j + 32], AX))
                link(dve.reduce_sum(dcov[:, 4:5], sums[:, :], AX))
                link(dve.tensor_scalar(dcov[:, :], dcov[:, :], 1.0 / (NB * L), None, ALU.mult))
                link(dve.tensor_tensor(c_mean, dcov[:, 4:5], c_nshift, ALU.subtract))
                mark["gathered"] = n[0]
                dve.wait_ge(S["pe_setup"], 2)
                link(dve.tensor_copy(q0[:, 0:20], psT[0:32, 0, 0:20]))

                def cov(i, j):
                    return q0[:, 5 * i + j:5 * i + j + 1]

                def mean(i):
                    return q0[:, 5 * i + 4:5 * i + 5]

                def low(i, j):
                    return q0[:, 20 + 4 * i + j:21 + 4 * i + j]

                def inv(i, j):
                    return q0[:, 36 + 4 * i + j:37 + 4 * i + j]

                def mix(k, i):
                    return q0[:, 52 + 4 * k + i:53 + 4 * k + i]

                tmp, pivot, root = q0[:, 88:89], q0[:, 89:90], q0[:, 90:91]
                for i in range(4):
                    for j in range(i + 1):
                        link(dve.tensor_tensor(tmp, mean(i), mean(j), ALU.mult))
                        link(dve.tensor_tensor(cov(i, j), cov(i, j), tmp, ALU.subtract))
                for j in range(4):
                    link(dve.tensor_scalar(pivot, cov(j, j), EPS0, None, ALU.add))
                    for k in range(j):
                        link(dve.tensor_tensor(tmp, low(j, k), low(j, k), ALU.mult))
                        link(dve.tensor_tensor(pivot, pivot, tmp, ALU.subtract))
                    mark["pivot", j] = n[0]
                    dve.wait_ge(S["stats_act"], j + 1)
                    link(dve.reciprocal(inv(j, j), root))
                    for i in range(j + 1, 4):
                        link(dve.tensor_copy(low(i, j), cov(i, j)))
                        for k in range(j):
                            link(dve.tensor_tensor(tmp, low(i, k), low(j, k), ALU.mult))
                            link(dve.tensor_tensor(low(i, j), low(i, j), tmp, ALU.subtract))
                        link(dve.tensor_tensor(low(i, j), low(i, j), inv(j, j), ALU.mult))
                for j in range(4):
                    for i in range(j + 1, 4):
                        link(dve.tensor_tensor(inv(i, j), low(i, j), inv(j, j), ALU.mult))
                        for k in range(j + 1, i):
                            link(dve.tensor_tensor(tmp, low(i, k), inv(k, j), ALU.mult))
                            link(dve.tensor_tensor(inv(i, j), inv(i, j), tmp, ALU.add))
                        link(dve.scalar_tensor_tensor(out=inv(i, j), in0=inv(i, j), scalar=-1.0, in1=inv(i, i),
                                                      op0=ALU.mult, op1=ALU.mult))
                for k in range(4):
                    for i in range(4):
                        link(dve.tensor_tensor(mix(k, i), w0s[:, i, k:k + 1], inv(k, k), ALU.mult))
                        for j in range(k + 1, 4):
                            link(dve.tensor_tensor(tmp, w0s[:, i, j:j + 1], inv(j, k), ALU.mult))
                            link(dve.tensor_tensor(mix(k, i), mix(k, i), tmp, ALU.add))
                mark["mixed"] = n[0]
                dve.wait_ge(S["pe_setup"], 3)
                link(dve.tensor_copy(wcol[:, :], psT[:, 1, 0:4]))
                for i in range(4):
                    link(dve.tensor_scalar(m0[:, 32 * i:32 * i + 32], mask32[:, :], wcol[:, i:i + 1], None, ALU.mult))
                mark["m0"] = n[0]
                dve.wait_ge(S["pe_setup"], 4)
                link(dve.tensor_tensor(c_c0, c_b0, psY[:, 0, 0:1], ALU.subtract))
                link(dve.tensor_tensor(c_c0g, c_c0, c_gbv, ALU.add))
                link(dve.tensor_copy(m0_rows[:, :], psY[:, 1, 0:128]))
                mark["m0_rows"] = n[0]
                dve.wait_ge(S["pe_setup"], 5)
                link(dve.tensor_copy(m0c[:, :], psT[:, 0, 0:128]))
                link(dve.tensor_copy(c_cc, psT[:, 1, 0:1]))
                mark["m0_done"] = n[0]

                def front(fb, fc, r):
                    for h, t in {AT_X + 1: [(0, 1), (0, 2)], AT_X + 3: [(0, 3), (1, 1)],
                                 AT_X + 4: [(1, 2), (1, 3)]}.get(r, []):
                        wait(dve, "tap0", fb, NH * fc + h + 1)
                        wait(dve, "conv", fb, (KC - 1) * (NH * fc + h) + t - 1)
                        dve.scalar_tensor_tensor(out=xc[:, h, cols(fc)], in0=xi[:, h, fc * CH + t:fc * CH + t + CH],
                                                 scalar=taps[:, h, t:t + 1], in1=xc[:, h, cols(fc)],
                                                 op0=ALU.mult, op1=ALU.add).then_inc(S["conv"], 1)
                    if r == AT_Z + 2:
                        wait(dve, "r1_ok", fb, fc + 1)
                        dve.tensor_copy(mid[2 * BCR:NROW, :], rem[2 * BCR:NROW, 0, :]).then_inc(S["mid_ok"], 1)
                    if r == AT_Z + 3:
                        wait(dve, "mid_ok", fb, fc + 1)
                        dve.tensor_tensor(rem[2 * BCR:NROW, 1, :], rem[2 * BCR:NROW, 0, :], mid[2 * BCR:NROW, :],
                                          ALU.subtract).then_inc(S["r2_ok"], 1)
                    if r == AT_Z + 4:
                        wait(dve, "r2_ok", fb, fc + 1)
                        dve.tensor_copy(bc[2 * BCR:NROW, cols(fc)], rem[2 * BCR:NROW, 1, :]).then_inc(S["low_ok"], 1)

                def normed(fb, fc):
                    wait(dve, "rs_ok", fb, fc + 1)
                    wait(dve, "xcen_ok", fb, fc + 1)
                    dve.tensor_tensor(xn[:, :], xcen[:, :], rstd[:, :], ALU.mult).then_inc(S["xn_ok"], 1)

                def rows(fb, fc):
                    wait(dve, "dbl_mm", fb, fc + 1)
                    dve.tensor_copy(dts[NROW:NROW + DR, :], psE[NROW:NROW + DR, 0, :]).then_inc(S["dt_ok"], 1)
                    wait(dve, "hi_ok", fb, fc + 1)
                    dve.tensor_tensor(rem[0:NROW, 0, :], psE[0:NROW, 0, :], bc[0:NROW, cols(fc)], ALU.subtract
                                      ).then_inc(S["r1_ok"], 1)

                def inputs(b, k):
                    ch, sl = k // NS, k % 2
                    wait(dve, "b_mm", b, k + 1)
                    if k % NS == 0:
                        wait(dve, "du_ok", b, NH * (ch + 1))
                    wait(dve, "h_ok", b, 2 * (k - 1))
                    dve.tensor_tensor(dbu[:, sl, :, :], psR[:, :].unsqueeze(1).to_broadcast([128, NH, CH]),
                                      du[:, :, cols(ch)], ALU.mult).then_inc(S["dbu_ok"], 1)

                def scans(b, k):
                    ch, n_ = divmod(k, NS)
                    sl = k % 2
                    wait(dve, "prod", b, k - 1)
                    wait(dve, "hlast_ok", b, min(k - 1, NS))
                    if ch:
                        wait(dve, "hlast_ok", b, n_ + 1)
                    wait(dve, "dbu_ok", b, k + 1)
                    for h in range(NH):
                        wait(dve, "da_ok", b, 2 * k + h + 1)
                        dve.tensor_tensor_scan(hs[:, sl, h, :], da[:, sl, h, :], dbu[:, sl, h, :],
                                               hlast[:, n_, h:h + 1] if ch else 0.0, ALU.mult, ALU.add
                                               ).then_inc(S["h_ok"], 1)

                def gate(b, ch):
                    wait(dve, "pair_mm", b, NS // 2 * (ch + 1))
                    dve.tensor_tensor(g[:, :, cols(ch)], psY[:, :, :], sz[:, :, cols(ch)], ALU.mult
                                      ).then_inc(S["g_ok"], 1)

                def normalise(a, o):
                    if o - 1 in TILE_STEP:
                        m, t = TILE_STEP[o - 1]
                        i = TILES * m + t
                        sl = i % 2
                        wait(dve, "p_ok", a, i + 1)
                        dve.reciprocal(rinv[:, sl:sl + 1], rsum[:, sl:sl + 1]).then_inc(S["rinv_ok"], 1)
                        wait(dve, "rinv_ok", a, i + 1)
                        dve.tensor_scalar(p[:, sl, :], p[:, sl, :], rinv[:, sl:sl + 1], None, ALU.mult
                                          ).then_inc(S["pn_ok"], 1)

                def query(a):
                    wait(dve, "q_mm", a, 1)
                    dve.tensor_scalar(qa[:, :], flat(psE), c_bq, None, ALU.add).then_inc(S["q_ok"], 1)

                def row_max(a, o):
                    if o in TILE_STEP:
                        m, t = TILE_STEP[o]
                        i = TILES * m + t
                        wait(dve, "e_mm", a, i + 1)
                        wait(dve, "p_ok", a, i - 1)
                        dve.tensor_reduce(nm[:, i % 2:i % 2 + 1], flat(psE), AX, ALU.max, negate=True
                                          ).then_inc(S["nm_ok"], 1)

                def attended(a, o):
                    if o - 3 in TILE_STEP and TILE_STEP[o - 3][1] % GT == GT - 1:
                        m, t = TILE_STEP[o - 3]
                        gq = t // GT
                        i = NG // 2 * m + gq
                        part = slice(gq * GL, (gq + 1) * GL)
                        wait(dve, "av_mm", a, i + 1)
                        if m == 0:
                            if gq == 0:
                                at(dve, "x2_out", a * 16)
                            wait(dve, "x1g_ok", a, NCH)
                            dve.scalar_tensor_tensor(out=x2[:, part], in0=psA[:, 0:GL], scalar=c_gam, in1=x1g[:, part],
                                                     op0=ALU.mult, op1=ALU.add).then_inc(S["out_ok"], 1)
                        else:
                            if gq == 0:
                                at(dve, "f_out", a * 16)
                            dve.tensor_copy(fa[:, part], psA[:, 0:GL]).then_inc(S["out_ok"], 1)
                            wait(dve, "out_ok", a, i + 1)
                            dve.bn_stats(bst[:, bass.ds(a, 1), gq, :].rearrange("p a s -> p (a s)"), fa[:, part]
                                         ).then_inc(S["bn_ok"], 1)

                def image(b, scan, more, att, late):
                    for c in range(NCH):
                        for r in range(NS):
                            k = NS * c + r
                            now = [(b - 1, k)] if att else []
                            if late and k < LATE:
                                now.append((b - 2, 2 * NS + k))
                            if scan:
                                inputs(b, k)
                            front_of = (b, 1) if c == 0 and scan else (b + 1, 0) if c == 1 and more else None
                            if front_of and r == AT_C + 3:
                                normed(*front_of)
                            if front_of and r == AT_Z + 2:
                                rows(*front_of)
                            for a, o in now:
                                normalise(a, o)
                            if att and k == 2:
                                gate(b - 1, 1)
                            if scan and k == NS + 2:
                                gate(b, 0)
                            if front_of and r == AT_Z:
                                front(*front_of, r)
                            if scan:
                                scans(b, k)
                            if att and k == AT_Q + 1:
                                query(b - 1)
                            if front_of and r != AT_Z:
                                front(*front_of, r)
                            for a, o in now:
                                row_max(a, o)
                                attended(a, o)

                for r in range(NS):
                    if r == AT_C + 3:
                        normed(0, 0)
                    if r == AT_Z + 2:
                        rows(0, 0)
                    front(0, 0, r)
                image(0, True, True, False, False)
                image(1, True, True, True, False)
                with dve.Fori(2, NB - 1) as b:
                    image(b, True, True, True, True)
                image(NB - 1, True, False, True, True)
                image(NB, False, False, True, True)
                image(NB + 1, False, False, False, True)

                wait(dve, "bn_ok", NB, 0)
                n[0] = 0
                link(dve.bn_aggr(mv[:, :], bst[:, :, :, :].rearrange("p b q s -> p (b q s)")), "fin_chain")
                link(dve.tensor_scalar(c_v2, mv[:, 1:2], EPS_BN, None, ALU.add), "fin_chain")
                dve.wait_ge(S["fin_act"], 1)
                link(dve.reciprocal(c_rs, c_rs), "fin_chain")
                link(dve.tensor_tensor(c_s, c_rs, c_bng, ALU.mult), "fin_chain")
                link(dve.tensor_tensor(c_t, mv[:, 0:1], c_s, ALU.mult), "fin_chain")
                link(dve.tensor_tensor(c_t, c_bnb, c_t, ALU.subtract), "fin_chain")

                def fin(i):
                    for k in range(SLOTS):
                        at(dve, "fscaled", i * SLOTS + k + 1)
                        dve.tensor_tensor(fbuf[k], fbuf[k], xbuf[k], ALU.add).then_inc(S["fsum"], 1)

                fin(0)
                with dve.Fori(1, ROUNDS) as i:
                    fin(i)

            @block.scalar
            def _(act):
                act.wait_ge(S["weights_in"], 16 * len(PARAMS))
                act.wait_ge(S["xl0"], 16)
                act.activation(x1[:, :], xin[:, :], ACT.Copy, accum_out=c_mean).then_inc(S["mean0"], 1)
                act.activation(neg_a[:, :, :], neg_a[:, :, :], ACT.Exp).then_inc(S["mean0"], 1)
                act.wait_ge(S["mean0"], 3)

                def centre(i, k):
                    n = i * 4 + k
                    at(act, f"xl{k}", (i + 1) * 16)
                    at(act, "st_turned", 2 * (n - 1))
                    act.activation(centred[k % 2][:, :], slots[k][:, :], ACT.Identity, bias=c_nshift,
                                   accum_out=sums[:, bass.ds(n, 1)]).then_inc(S["st_centred"], 1)

                for k in range(4):
                    centre(0, k)
                with act.Fori(1, NB // 4) as i:
                    for k in range(4):
                        centre(i, k)

                for j in range(4):
                    act.wait_ge(S["stats_chain"], mark["pivot", j])
                    act.sqrt(q0[:, 90:91], q0[:, 89:90]).then_inc(S["stats_act"], 1)
                act.wait_ge(S["stats_chain"], mark["m0_done"])

                def front(fb, fc, r):
                    if r == AT_C:
                        wait(act, "cent_mm", fb, fc + 1)
                        wait(act, "xn_ok", fb, fc)
                        act.activation(xcen[:, :], psT[:, 0, :], ACT.Identity, bias=c_cc).then_inc(S["xcen_ok"], 1)
                        act.activation(sq[:, :], psT[:, 0, :], ACT.Square, bias=c_cc).then_inc(S["sq_ok"], 1)
                    if r == AT_C + 2:
                        wait(act, "var_mm", fb, fc + 1)
                        act.activation(lnv[:, :], psE[:, 0, :], ACT.Ln, bias=c_v).then_inc(S["lnv_ok"], 1)
                        wait(act, "lnv_ok", fb, fc + 1)
                        act.activation(rstd[:, :], lnv[:, :], ACT.Exp, scale=-0.5).then_inc(S["rs_ok"], 1)
                    if r == AT_X:
                        for h in range(NH):
                            wait(act, "xi_mm", fb, 2 * fc + h + 1)
                            lo = KC - 1 + fc * CH
                            act.activation(xi[:, h, lo:lo + CH], psT[:, h, :], ACT.Identity, bias=c_wb[:, h:h + 1]
                                           ).then_inc(S["xi_ok"], 1)
                    if r in (AT_X, AT_X + 1):
                        h = r - AT_X
                        wait(act, "pair_mm", fb - 1, NS // 2 * (fc + 1))
                        wait(act, "xi_ok", fb, 2 * fc + h + 1)
                        act.activation(xc[:, h, cols(fc)], xi[:, h, fc * CH:fc * CH + CH], ACT.Identity,
                                       bias=c_cb[:, h:h + 1], scale=taps[:, h, 0:1]).then_inc(S["tap0"], 1)
                    if r == AT_Z:
                        for h in range(NH):
                            wait(act, "conv", fb, (KC - 1) * (NH * fc + h + 1))
                            act.activation(xc[:, h, cols(fc)], xc[:, h, cols(fc)], ACT.Silu).then_inc(S["xc_ok"], 1)
                        for h in range(NH):
                            wait(act, "z_mm", fb, 2 * fc + h + 1)
                            act.activation(sz[:, h, cols(fc)], psT[:, h, :], ACT.Silu, bias=c_wb[:, NH + h:NH + h + 1]
                                           ).then_inc(S["z_ok"], 1)
                    if r == AT_Z + 1:
                        wait(act, "dbl_mm", fb, fc + 1)
                        act.activation(bc[0:NROW, cols(fc)], psE[0:NROW, 0, :], ACT.Copy).then_inc(S["hi_ok"], 1)
                        act.preload_act_table_set("natural_log_exp_and_others")
                    if r in (AT_P, AT_P + 1):
                        h = r - AT_P
                        wait(act, "dpre_mm", fb, 2 * fc + h + 1)
                        act.activation(sp_e[:, h, :], psT[:, h, :], ACT.Abs, bias=c_bdt[:, h:h + 1]
                                       ).then_inc(S["sp_abs"], 1)
                        act.activation(delta[:, h, cols(fc)], psT[:, h, :], ACT.Relu, bias=c_bdt[:, h:h + 1]
                                       ).then_inc(S["sp_relu"], 1)
                    if r in (AT_P + 2, AT_P + 3):
                        h = r - AT_P - 2
                        wait(act, "sp_abs", fb, 2 * fc + h + 1)
                        act.activation(sp_e[:, h, :], sp_e[:, h, :], ACT.Exp, scale=-1.0).then_inc(S["sp_exp"], 1)
                        wait(act, "sp_exp", fb, 2 * fc + h + 1)
                        act.activation(sp_l[:, h, :], sp_e[:, h, :], ACT.Ln, bias=1.0).then_inc(S["sp_ln"], 1)

                def middle(fb, fc):
                    wait(act, "r1_ok", fb, fc + 1)
                    act.activation(bc[BCR:2 * BCR, cols(fc)], rem[BCR:2 * BCR, 0, :], ACT.Copy).then_inc(S["midb_ok"], 1)

                def decay(b, k):
                    ch, n = divmod(k, NS)
                    for h in range(NH):
                        if n == 0:
                            wait(act, "delta_ok", b, NH * ch + h + 1)
                        wait(act, "h_ok", b, 2 * (k - 2) + h + 1)
                        act.activation(da[:, k % 2, h, :], delta[:, h, cols(ch)], ACT.Exp,
                                       scale=neg_a[:, h, n:n + 1]).then_inc(S["da_ok"], 1)

                def c_row(b, k):
                    wait(act, "c_mm", b, k + 1)
                    wait(act, "prod", b, k - 1)
                    act.activation(cs[:, k % 2, :], psR[:, :], ACT.Copy).then_inc(S["c_ok"], 1)

                def turned_out(a, o):
                    if o - 1 in TILE_STEP:
                        m, t = TILE_STEP[o - 1]
                        i = TILES * m + t
                        for q in range(2):
                            wait(act, "turn", a, 2 * i + q + 1)
                            if t % GT == 0:
                                wait(act, "av_mm", a, i // GT - 1)
                            act.activation(pt[:, i // GT % 2, 4 * q:4 * q + 4, 128 * (t % GT):128 * (t % GT) + 128],
                                           psT[:, q, :].rearrange("p (j i) -> p j i", j=4), ACT.Copy
                                           ).then_inc(S["pt_ok"], 1)

                def key(a, m):
                    wait(act, "k_mm", a, m + 1)
                    if m == 0:
                        act.activation(ka[:, :], flat(psT), ACT.Identity, bias=c_bk).then_inc(S["k_ok"], 1)
                    else:
                        act.activation(ka[:, :], flat(psT), ACT.Copy).then_inc(S["k_ok"], 1)

                def value(a, m):
                    wait(act, "v_mm", a, m + 1)
                    act.activation(va[:, :, :], split(psT), ACT.Copy).then_inc(S["v_ok"], 1)

                def residual(b, ch):
                    wait(act, "x1_mm", b, ch + 1)
                    act.activation(x1[:, cols(ch)], psE[:, 1, :], ACT.Identity, bias=c_c0).then_inc(S["x1_ok"], 1)
                    wait(act, "out_ok", b - 1, NG // 4 * (ch + 1))
                    act.activation(x1g[:, cols(ch)], psE[:, 1, :], ACT.Identity, bias=c_c0g).then_inc(S["x1g_ok"], 1)

                def numer(a, o):
                    if o in TILE_STEP:
                        m, t = TILE_STEP[o]
                        i = TILES * m + t
                        wait(act, "nm_ok", a, i + 1)
                        wait(act, "turn", a, 2 * (i - 1))
                        act.activation(p[:, i % 2, :], flat(psE), ACT.Exp, bias=nm[:, i % 2:i % 2 + 1],
                                       accum_out=rsum[:, i % 2:i % 2 + 1]).then_inc(S["p_ok"], 1)

                BEFORE_DECAY = (AT_C + 2, AT_Z + 1, AT_P + 1)

                def image(b, scan, more, att, late):
                    for c in range(NCH):
                        for r in range(NS):
                            k = NS * c + r
                            now = [(b - 1, k)] if att else []
                            if late and k < LATE:
                                now.append((b - 2, 2 * NS + k))
                            front_of = (b, 1) if c == 0 and scan else (b + 1, 0) if c == 1 and more else None
                            if att and r == AT_Q + 1:
                                key(b - 1, c)
                            if scan:
                                c_row(b, k)
                            if att and r == AT_V + 1:
                                value(b - 1, c)
                            for a, o in now:
                                if r == 1:
                                    turned_out(a, o)
                            if front_of and r in BEFORE_DECAY:
                                front(*front_of, r)
                            if scan and (k < STEPS - 1 or more):
                                decay(*((b, k + 1) if k < STEPS - 1 else (b + 1, 0)))
                            if att and k == AT_R:
                                residual(b - 1, 1)
                            if scan and k == NS + AT_R:
                                residual(b, 0)
                            if front_of and r not in BEFORE_DECAY and r != AT_P:
                                front(*front_of, r)
                            if front_of and r == AT_Z + 2:
                                middle(*front_of)
                            for a, o in now:
                                if r != 1:
                                    turned_out(a, o)
                            for a, o in now:
                                numer(a, o)
                            if front_of and r == AT_P:
                                front(*front_of, r)

                for r in range(NS):
                    front(0, 0, r)
                    if r == AT_Z + 1:
                        middle(0, 0)
                decay(0, 0)
                image(0, True, True, False, False)
                image(1, True, True, True, False)
                with act.Fori(2, NB - 1) as b:
                    image(b, True, True, True, True)
                image(NB - 1, True, False, True, True)
                image(NB, False, False, True, True)
                image(NB + 1, False, False, False, True)

                act.wait_ge(S["fin_chain"], 2)
                act.sqrt(c_rs, c_v2).then_inc(S["fin_act"], 1)
                act.wait_ge(S["fin_chain"], 6)

                def images(dram, i, k):
                    return dram[bass.ds(2 * (i * SLOTS + k), 2), :, :].rearrange("a c l -> c a l")

                def fin(i):
                    for k in range(SLOTS):
                        at(act, f"fl{k}", 32 * (i + 1))
                        act.activation(fbuf[k], fbuf[k], ACT.Identity, bias=c_t, scale=c_s).then_inc(S["fscaled"], 1)
                        if k:
                            store(i, k - 1)
                    store(i, SLOTS - 1)

                def store(i, k):
                    at(act, "fsum", i * SLOTS + k + 1)
                    act.dma_start(images(out, i, k), fbuf[k]).then_inc(S[f"out{k}"], 16)

                fin(0)
                with act.Fori(1, ROUNDS) as i:
                    fin(i)

            @block.tensor
            def _(pe):
                def mm(dst, lhsT, rhs, start=True, stop=True):
                    return pe.matmul(dst, lhsT, rhs, start=start, stop=stop)

                def wide(dst, lhsT, rhs, rows=128):
                    for c in range(NCH):
                        last = mm(dst[0:rows, c, :], lhsT, rhs[:, c * CH:(c + 1) * CH])
                    return last

                pe.wait_ge(S["weights_in"], 16 * len(PARAMS))
                pe.wait_ge(S["consts_made"], mark["consts"])
                for e in range(4):
                    last = mm(psY[:, 0, e:e + 1], w_in_t[:, 128 * e:128 * e + 128], c_lnb)
                mm(psA[:, 0:C], ph_r[:, :], th_r[:, :]).then_inc(S["pe_setup"], 1)

                def st_turn(m, k, q):
                    at(pe, "st_centred", m + 1)
                    at(pe, "st_copied", 2 * (m - 1) + q + 1)
                    for j in range(4):
                        last = pe.transpose(psT[:, q, 128 * j:128 * j + 128],
                                            centred[k][:, (4 * q + j) * 128:(4 * q + j + 1) * 128], ident[:, :])
                    last.then_inc(S["st_turned"], 1)

                def st_gram(m, q, start=False, stop=False):
                    at(pe, "st_copied", 2 * m + q + 1)
                    for j in range(4):
                        blk = turned[q][:, 128 * j:128 * j + 128]
                        last = mm(psR[:, 0:128], blk, blk, start=start and j == 0, stop=stop and j == 3)
                    last.then_inc(S["st_gram"], 1)

                def stat(m, k, start=False):
                    for q in range(2):
                        st_turn(m + 1, 1 - k, q)
                        st_gram(m, q, start=start and q == 0)

                st_turn(0, 0, 0)
                st_turn(0, 0, 1)
                stat(0, 0, True)
                with pe.Fori(0, NB // 2 - 1) as i:
                    stat(i * 2 + 1, 1)
                    stat(i * 2 + 2, 0)
                st_gram(NB - 1, 0)
                st_gram(NB - 1, 1, stop=True)
                pe.wait_ge(S["stats_chain"], mark["gathered"])
                for i in range(4):
                    last = mm(psT[0:32, 0, 5 * i:5 * i + 5], ident[:, 32 * i:32 * i + 32], dcov[:, :])
                last.then_inc(S["pe_setup"], 1)
                pe.wait_ge(S["stats_chain"], mark["mixed"])
                for k in range(4):
                    last = mm(psT[32 * k:32 * k + 32, 1, 0:4], ident[0:32, 0:32], q0[:, 52 + 4 * k:56 + 4 * k])
                last.then_inc(S["pe_setup"], 1)
                pe.wait_ge(S["stats_chain"], mark["m0"])
                pe.transpose(psY[:, 1, 0:128], m0[:, :], ident[:, :])
                mm(psY[:, 0, 0:1], m0[:, :], c_mean).then_inc(S["pe_setup"], 1)
                pe.wait_ge(S["stats_chain"], mark["m0_rows"])
                mm(psT[:, 0, 0:128], m0_rows[:, :], cent[:, :])
                mm(psT[:, 1, 0:1], cent[:, :], c_c0).then_inc(S["pe_setup"], 1)
                pe.wait_ge(S["stats_chain"], mark["m0_done"])

                def front(what, fb, fc, att):
                    if what == "centre":
                        at(pe, "x_in", 16 * (fb + 1))
                        wait(pe, "sp_relu", fb, 2 * fc)
                        if att:
                            wait(pe, "pt_ok", *att["turned7"])
                        mm(psT[:, 0, :], m0c[:, :], xin[:, cols(fc)]).then_inc(S["cent_mm"], 1)
                    if what == "gates":
                        if att:
                            wait(pe, "pt_ok", *att["turned1"])
                        else:
                            wait(pe, "xi_ok", fb, 2 * fc + 2)
                        for h in range(NH):
                            mm(psT[:, h, :], w_in_t[:, DI + C * h:DI + C * h + C], xn[:, :]).then_inc(S["z_mm"], 1)
                    if what == "steps":
                        wait(pe, "dt_ok", fb, fc + 1)
                        wait(pe, "z_ok", fb, 2 * fc + 2)
                        for h in range(NH):
                            mm(psT[:, h, :], w_dt_t[NROW:NROW + DR, C * h:C * h + C], dts[NROW:NROW + DR, :]
                               ).then_inc(S["dpre_mm"], 1)
                    if what == "variance":
                        wait(pe, "sq_ok", fb, fc + 1)
                        if att:
                            wait(pe, "p_ok", *att["tile7"])
                        mm(psE[:, 0, :], avg[:, :], sq[:, :]).then_inc(S["var_mm"], 1)
                    if what == "inner":
                        wait(pe, "xn_ok", fb, fc + 1)
                        if att:
                            wait(pe, "k_ok", *att["k"])
                        for h in range(NH):
                            mm(psT[:, h, :], w_in_t[:, C * h:C * h + C], xn[:, :]).then_inc(S["xi_mm"], 1)
                    if what == "rows":
                        wait(pe, "xc_ok", fb, 2 * fc + 2)
                        if att:
                            wait(pe, "p_ok", *att["tile1"])
                        for h in range(NH):
                            last = mm(psE[0:NROW + DR, 0, :], w_x_t[:, h, :], xc[:, h, cols(fc)],
                                      start=(h == 0), stop=(h == NH - 1))
                        last.then_inc(S["dbl_mm"], 1)

                def b_row(b, k):
                    ch, n_ = divmod(k, NS)
                    if n_ == 0:
                        wait(pe, "low_ok", b, ch + 1)
                        wait(pe, "midb_ok", b, ch + 1)
                    wait(pe, "c_ok", b, k)
                    mm(psR[:, :], sel[0:NROW, n_, :], bc[0:NROW, cols(ch)]).then_inc(S["b_mm"], 1)

                def c_row(b, k):
                    ch, n_ = divmod(k, NS)
                    wait(pe, "dbu_ok", b, k + 1)
                    mm(psR[:, :], sel[0:NROW, NS + n_, :], bc[0:NROW, cols(ch)]).then_inc(S["c_mm"], 1)

                def sum_states(b, k):
                    pr, h = k // 2 - 1, k % 2
                    ch, q = divmod(pr, NS // 2)
                    if q == 0 and h == 0:
                        wait(pe, "g_ok", b, ch)
                    wait(pe, "pair", b, pr + 1)
                    last = mm(psY[:, h, :], ident[:, :], pa[:, pr % 2, h, :], start=(q == 0), stop=(q == NS // 2 - 1))
                    if h == 1:
                        last.then_inc(S["pair_mm"], 1)

                def skip_term(b, ch, h):
                    wait(pe, "xc_ok", b, NH * ch + h + 1)
                    mm(psY[:, h, :], dp_diag[:, h, :], xc[:, h, cols(ch)], start=False, stop=False)

                def residual(b, ch, front, late):
                    wait(pe, "g_ok", b, ch + 1)
                    at(pe, f"xr_in{ch}", 16 * (b + 1))
                    if late:
                        wait(pe, "p_ok", *late)
                    mm(psE[:, 1, :], m0[:, :], xres[:, cols(ch)], stop=False)
                    for h in range(NH):
                        last = mm(psE[:, 1, :], w_out_t[:, h, :], g[:, h, cols(ch)], start=False, stop=(h == NH - 1))
                    last.then_inc(S["x1_mm"], 1)

                def energy(a, m, t, front, scan):
                    i = TILES * m + t
                    queries = (qa, x2)[m]
                    if t == 0:
                        wait(pe, "q_ok", a, 1)
                        wait(pe, "k_ok", a, m + 1)
                        if m == 1 and front:
                            wait(pe, "lnv_ok", front[0], front[1] + 1)
                        if m == 1 and scan:
                            wait(pe, "x1g_ok", a + 1, 1)
                    if t == 2 and front:
                        for name in ("hi_ok", "dt_ok", "r1_ok"):
                            wait(pe, name, front[0], front[1] + 1)
                    wait(pe, "p_ok", a, i)
                    for c in range(NCH):
                        last = mm(psE[:, c, :], queries[:, 128 * t:128 * t + 128], ka[:, cols(c)])
                    last.then_inc(S["e_mm"], 1)

                def turn(a, m, t, front):
                    i = TILES * m + t
                    wait(pe, "pn_ok", a, i + 1)
                    if t == 0:
                        wait(pe, "v_ok", a, m + 1)
                    if t == 2 and front:
                        wait(pe, "sp_relu", front[0], 2 * front[1] + 2)
                    for q in range(2):
                        wait(pe, "pt_ok", a, 2 * (i - 1) + q + 1)
                        for j in range(4):
                            last = pe.transpose(psT[:, q, 128 * j:128 * j + 128],
                                                p[:, i % 2, (4 * q + j) * 128:(4 * q + j + 1) * 128], ident[:, :])
                        last.then_inc(S["turn"], 1)

                def values(a, m, t, half):
                    i = (TILES * m + t) // GT
                    if half == 0:
                        wait(pe, "out_ok", a, i)
                    wait(pe, "pt_ok", a, 2 * GT * (i + 1) - 1 + half)
                    for j in range(TB // 2 * half, TB // 2 * (half + 1)):
                        last = mm(psA[:, 0:GL], va[:, j, :], pt[:, i % 2, j, :], start=(j == 0), stop=(j == TB - 1))
                    if half:
                        last.then_inc(S["av_mm"], 1)

                def project(a, m, c, front, other):
                    if m == 0:
                        wait(pe, "x1_ok", a, c + 1)
                    else:
                        wait(pe, "out_ok", a, (c + 1) * NG // 4)
                    if c == 0 and m == 0 and other:
                        wait(pe, "pt_ok", a - 1, 4 * TILES)
                    if m == 1:
                        wait(pe, "pt_ok", a, 2 * TILES)
                    last = mm(psT[:, c, :], (w_k_t, tp_t)[m][:, :], (x1, x2)[m][:, cols(c)])
                    if c == NCH - 1:
                        last.then_inc(S["k_mm"], 1)
                    if m == 0:
                        if c == 0 and front:
                            wait(pe, "lnv_ok", front[0], front[1] + 1)
                        if c == 1:
                            wait(pe, "x1g_ok", a, NCH)
                        last = mm(psE[:, c, :], w_q_t[:, :], x1[:, cols(c)])
                        if c == NCH - 1:
                            last.then_inc(S["q_mm"], 1)

                def project_values(a, m, front):
                    if front:
                        wait(pe, "xi_ok", front[0], 2 * front[1] + 2)
                    wait(pe, "k_ok", a, m + 1)
                    src, w = ((x1, w_v_t), (x2, cv_t))[m]
                    for j in range(TB):
                        last = mm(split(psT)[:, j, :], src[:, 128 * j:128 * j + 128], w[:, :])
                    last.then_inc(S["v_mm"], 1)

                ORDER = [
                    ("weigh", "energy", "turn add"),
                    ("weigh", "turn", "add"),
                    ("centre", "weigh", "weigh_rest add"),
                    ("", "residual", "add variance"),
                    ("", "project0", "add project1"),
                    ("", "add", "inner"),
                    ("", "energy", "project_values add"),
                    ("", "energy", "turn add"),
                    ("", "skip0", "turn add"),
                    ("gates", "add", "weigh"),
                    ("weigh", "rows", "add"),
                    ("", "add energy", "steps"),
                    ("", "energy", "turn skip1 add"),
                    ("", "energy", "turn add"),
                    ("weigh", "energy", "turn add"),
                    ("weigh", "energy", "turn add"),
                ]
                FRONT = ("centre", "variance", "inner", "gates", "rows", "steps")

                def image(b, scan, more, att, late):
                    for c in range(NCH):
                        if c == 0:
                            front_of = (b, 1) if scan else None
                            old = (b - 2, 1) if late else None
                        else:
                            front_of = (b + 1, 0) if more else None
                            old = (b - 1, 0) if att else None
                        beside = {}
                        if old:
                            beside.update(turned7=(old[0], 16 * old[1] + 16), tile7=(old[0], 8 * old[1] + 8))
                        if att:
                            beside.update(k=(b - 1, c + 1), turned1=(b - 1, 16 * c + 4), tile1=(b - 1, 8 * c + 2))
                        for r in range(NS):
                            k = NS * c + r
                            now = [(b - 1, k)] if att else []
                            if late and k < LATE:
                                now.append((b - 2, 2 * NS + k))
                            need = beside if (old if r in (AT_C, AT_R) else att) else None

                            def work(names):
                                for what in names.split():
                                    if what in FRONT:
                                        if front_of:
                                            front(what, *front_of, need)
                                    elif what == "add":
                                        if scan and k >= 2:
                                            sum_states(b, k)
                                        elif att and k < 2:
                                            sum_states(b - 1, STEPS + k)
                                    elif what in ("skip0", "skip1"):
                                        if scan:
                                            skip_term(b, c, int(what == "skip1"))
                                    elif what == "residual":
                                        if att and c == 0:
                                            residual(b - 1, 1, front_of, (b - 2, 16) if late else None)
                                        if scan and c == 1:
                                            residual(b, 0, front_of, (b - 1, 8) if att else None)
                                    elif what in ("project0", "project1"):
                                        if att:
                                            project(b - 1, c, int(what == "project1"), front_of, late if c == 0 else scan)
                                    elif what == "project_values":
                                        if att:
                                            project_values(b - 1, c, front_of)
                                    for a, o in now:
                                        if what == "energy" and o in TILE_STEP:
                                            energy(a, *TILE_STEP[o], front_of, scan)
                                        if what == "turn" and o - 1 in TILE_STEP:
                                            turn(a, *TILE_STEP[o - 1], front_of)
                                        for half in range(2):
                                            last_tile = o - 2 - (half if what == "weigh" else 0)
                                            if (what == "weigh" or what == "weigh_rest" and half) and last_tile in TILE_STEP and TILE_STEP[last_tile][1] % GT == GT - 1:
                                                values(a, *TILE_STEP[last_tile], half)

                            before, between, after = ORDER[r]
                            work(before)
                            if scan:
                                c_row(b, k)
                            work(between)
                            if scan and (k < STEPS - 1 or more):
                                b_row(*((b, k + 1) if k < STEPS - 1 else (b + 1, 0)))
                            work(after)

                for what in FRONT:
                    front(what, 0, 0, None)
                b_row(0, 0)
                image(0, True, True, False, False)
                image(1, True, True, True, False)
                with pe.Fori(2, NB - 1) as b:
                    image(b, True, True, True, True)
                image(NB - 1, True, False, True, True)
                image(NB, False, False, True, True)
                image(NB + 1, False, False, False, True)

            @block.sync
            def _(sp):
                for dst, src in PARAMS:
                    sp.dma_start(dst, src).then_inc(S["weights_in"], 16)

                def load_stat(i, k):
                    at(sp, "st_centred", i * 4 + k - 3)
                    sp.dma_start(slots[k][:, :], x[bass.ds(i * 4 + k, 1), :, :].rearrange("a c l -> c (a l)")
                                 ).then_inc(S[f"xl{k}"], 16)

                for k in range(4):
                    load_stat(0, k)
                with sp.Fori(1, NB // 4) as i:
                    for k in range(4):
                        load_stat(i, k)
                at(sp, "st_centred", NB)

                def load_x(b):
                    sp.dma_start(xin[:, :], x[bass.ds(b, 1), :, :].rearrange("a c l -> c (a l)")).then_inc(S["x_in"], 16)

                def load_residual(b, c):
                    sp.dma_start(xres[:, cols(c)], x[bass.ds(b, 1), :, cols(c)].rearrange("a c l -> c (a l)")
                                 ).then_inc(S[f"xr_in{c}"], 16)

                def image(b, scan, more, att, late):
                    if late:
                        wait(sp, "bn_ok", b - 2, NG // 2)
                        sp.dma_start(f_dram[bass.ds(b - 2, 1), :, :].rearrange("a c l -> c (a l)"), fa[:, :]
                                     ).then_inc(S["f_out"], 16)
                    if att and scan:
                        wait(sp, "x1_mm", b - 1, 2)
                        load_residual(b, 1)
                    if more:
                        wait(sp, "cent_mm", b, 2)
                        load_x(b + 1)
                    if scan:
                        wait(sp, "x1_mm", b, 1)
                        if more:
                            load_residual(b + 1, 0)
                    if att:
                        wait(sp, "out_ok", b - 1, NG // 2)
                        sp.dma_start(x2_dram[bass.ds(b - 1, 1), :, :].rearrange("a c l -> c (a l)"), x2[:, :]
                                     ).then_inc(S["x2_out"], 16)

                def images(dram, i, k):
                    return dram[bass.ds(2 * (i * SLOTS + k), 2), :, :].rearrange("a c l -> c a l")

                def load_fin(i):
                    for k in range(SLOTS):
                        at(sp, f"out{k}", 16 * i)
                        sp.dma_start(fbuf[k], images(f_dram, i, k)).then_inc(S[f"fl{k}"], 16)
                        sp.dma_start(xbuf[k], images(x2_dram, i, k)).then_inc(S[f"fl{k}"], 16)

                load_x(0)
                load_residual(0, 0)
                load_residual(0, 1)
                image(0, True, True, False, False)
                image(1, True, True, True, False)
                with sp.Fori(2, NB - 1) as b:
                    image(b, True, True, True, True)
                image(NB - 1, True, False, True, True)
                wait(sp, "x1_mm", NB, 0)
                at(sp, "f_out", 16 * 2 * SLOTS)
                at(sp, "x2_out", 16 * 2 * SLOTS)
                load_fin(0)
                image(NB, False, False, True, True)
                image(NB + 1, False, False, False, True)
                at(sp, "f_out", 16 * NB)
                at(sp, "x2_out", 16 * NB)

                with sp.Fori(1, ROUNDS) as i:
                    load_fin(i)
                for k in range(SLOTS):
                    at(sp, f"out{k}", 16 * ROUNDS)


def kernel(x, L0_conv_weight, L0_conv_bias, L1_conv_ln_w, L1_conv_ln_b, L1_conv_W_in, L1_conv_conv_w, L1_conv_conv_b,
           L1_conv_W_x, L1_conv_W_dt, L1_conv_b_dt, L1_conv_A_log, L1_conv_Dp, L1_conv_W_out, L2_conv_Wq, L2_conv_bq,
           L2_conv_Wk, L2_conv_bk, L2_conv_Wv, L2_conv_bv, L2_conv_gamma, L3_conv_theta_w, L3_conv_phi_w, L3_conv_conv_w,
           L3_conv_gamma, L3_conv_beta):
    import numpy as np
    import concourse.bacc as bacc
    from concourse.bass_utils import run_bass_kernel_spmd

    def col(v):
        return np.asarray(v).reshape(C, 1)

    def halves(v):
        v = np.asarray(v).reshape(NH, C, -1).transpose(1, 0, 2)
        return v

    arrays = dict(
        x=np.asarray(x).reshape(NB, C, L),
        w0=np.asarray(L0_conv_weight).transpose(2, 0, 1), b0=col(L0_conv_bias), ln_w=col(L1_conv_ln_w), ln_b=col(L1_conv_ln_b),
        w_in=np.asarray(L1_conv_W_in).T, conv_w=halves(L1_conv_conv_w), conv_b=halves(L1_conv_conv_b)[:, :, 0],
        w_x=halves(np.asarray(L1_conv_W_x).T), w_dt=np.asarray(L1_conv_W_dt).T, b_dt=halves(L1_conv_b_dt)[:, :, 0],
        a_log=halves(L1_conv_A_log), dp=halves(L1_conv_Dp)[:, :, 0], w_out=halves(np.asarray(L1_conv_W_out).T),
        w_q=np.asarray(L2_conv_Wq).T, b_q=col(L2_conv_bq), w_k=np.asarray(L2_conv_Wk).T, b_k=col(L2_conv_bk),
        w_v=np.asarray(L2_conv_Wv).T, b_v=col(L2_conv_bv), gam=np.asarray(L2_conv_gamma).reshape(1, 1),
        th_w=np.asarray(L3_conv_theta_w), ph_w=np.asarray(L3_conv_phi_w), cv_w=np.asarray(L3_conv_conv_w).T,
        bn_g=col(L3_conv_gamma), bn_b=col(L3_conv_beta),
    )
    arrays = {k: np.ascontiguousarray(v) for k, v in arrays.items()}
    nc = bacc.Bacc("TRN2", target_bir_lowering=False, num_devices=1)
    aps = {k: nc.dram_tensor(k, v.shape, mybir.dt.from_np(v.dtype), kind="ExternalInput").ap() for k, v in arrays.items()}
    out = nc.dram_tensor("out", (NB, C, L), mybir.dt.float32, kind="ExternalOutput").ap()
    build(nc, out=out, **aps)
    result = run_bass_kernel_spmd(nc, [arrays], core_ids=[0])
    return result.results[0]["out"].reshape(NB, C, HH, WW)
```
